# Optimizing a Trainium2 kernel written in Bass

```python
import numpy as np
import jax
import jax.numpy as jnp

def _softmax(x, axis=-1):
    return jax.nn.softmax(x, axis=axis)

def _gelu(x):
    return jax.nn.gelu(x, approximate=True)

def _silu(x):
    return jax.nn.silu(x)

def _sigmoid(x):
    return jax.nn.sigmoid(x)

def _layernorm(x, axis=-1, eps=1e-05):
    m = jnp.mean(x, axis=axis, keepdims=True)
    v = jnp.var(x, axis=axis, keepdims=True)
    return (x - m) / jnp.sqrt(v + eps)

def _scatter_add(tgt, idx, src, axis=0):
    return tgt.at[idx].add(src)

def _segment_sum(src, seg, n):
    return jax.ops.segment_sum(src, seg, n)
kernel_name = 'mk_conv_seq_d1_conv_nchw1024_r2_447b41'

def setup_inputs(seed: int=0):
    np.random.seed(seed)
    _w = jnp.asarray

    def _rec_inputs():
        import jax
        import jax.numpy as jnp
        _gk = jax.random.key(seed)
        x = -4.65e-05 + 0.9999 * jax.random.normal(jax.random.fold_in(_gk, 1), (8, 512, 32, 48), jnp.float32)
        return x
    x = _rec_inputs()

    def _L0_conv_setup():
        import jax, jax.numpy as jnp
        import numpy as np
        EPS = 1e-12
        key = jax.random.key(seed)
        k1, k2, k3, k4 = jax.random.split(key, 4)
        B, C, H, W_sp = (8, 512, 32, 48)
        N = 40
        x = jax.random.normal(k1, (B, C, H, W_sp), dtype=jnp.float32)
        centroids = jax.random.normal(k2, (N, C), dtype=jnp.float32)
        W = jax.random.normal(k3, (C, C), dtype=jnp.float32) * 0.02
        b = jax.random.normal(k4, (C,), dtype=jnp.float32) * 0.02
        return {'x': x, 'centroids': centroids, 'W': W, 'b': b}
    _L0_conv_all = _L0_conv_setup()
    _L0_conv_in = {k: v for k, v in _L0_conv_all.items() if k in ('centroids', 'W', 'b')}
    del _L0_conv_all
    return {'x': x, 'L0_conv_centroids': _L0_conv_in['centroids'], 'L0_conv_W': _L0_conv_in['W'], 'L0_conv_b': _L0_conv_in['b']}

def reference(x, L0_conv_centroids, L0_conv_W, L0_conv_b):
    import jax
    import jax.numpy as jnp

    def _L0_conv_ref(x, centroids, W, b):
        import jax, jax.numpy as jnp
        import numpy as np
        EPS = 1e-12
        N = centroids.shape[0]
        B = x.shape[0]
        xn = x / jnp.maximum(jnp.linalg.norm(x, axis=1, keepdims=True), EPS)
        cn = centroids / jnp.maximum(jnp.linalg.norm(centroids, axis=1, keepdims=True), EPS)
        sim = jnp.einsum('bchw,nc->bnhw', xn, cn)
        idx = jnp.argmax(sim, axis=1)
        onehot = jax.nn.one_hot(idx, N, dtype=x.dtype)
        sum_x = jnp.einsum('bhwn,bchw->bnc', onehot, x)
        count = jnp.sum(onehot, axis=(1, 2))
        centroids_local = sum_x / jnp.maximum(count, 1.0)[..., None]
        gathered = centroids_local[jnp.arange(B)[:, None, None], idx]
        delta = jnp.transpose(gathered, (0, 3, 1, 2)) - x
        alpha = jnp.exp(-jnp.mean(delta * delta, axis=1, keepdims=True))
        y = x + alpha * delta
        out = jnp.einsum('oc,bchw->bohw', W, y) + b[None, :, None, None]
        return jax.nn.relu(out)

    def _gn(v, G=32, eps=1e-05):
        B_, C_, H_, W_ = v.shape
        g = v.reshape(B_, G, C_ // G, H_, W_)
        m = jnp.mean(g, axis=(2, 3, 4), keepdims=True)
        s = jnp.var(g, axis=(2, 3, 4), keepdims=True)
        return ((g - m) / jnp.sqrt(s + eps)).reshape(v.shape)

    def _ln_c(v, eps=1e-06):
        m = jnp.mean(v, axis=1, keepdims=True)
        s = jnp.var(v, axis=1, keepdims=True)
        return (v - m) / jnp.sqrt(s + eps)

    def _ln_t(v, eps=1e-05):
        m = jnp.mean(v, axis=-1, keepdims=True)
        s = jnp.var(v, axis=-1, keepdims=True)
        return (v - m) / jnp.sqrt(s + eps)

    def _to_tokens(v):
        B_, C_, H_, W_ = v.shape
        return v.reshape(B_, C_, H_ * W_).transpose(0, 2, 1)

    def _from_tokens(t, like):
        B_, C_, H_, W_ = like.shape
        return t.transpose(0, 2, 1).reshape(B_, C_, H_, W_)
    x = _L0_conv_ref(x, L0_conv_centroids, L0_conv_W, L0_conv_b)
    return x

_drawn_inputs = setup_inputs


def setup_inputs(seed=0):
    import zlib

    import numpy as np

    out = dict(_drawn_inputs(seed))
    spreads = {}
    factors = {}
    for name, (base, spread) in spreads.items():
        noise = np.random.default_rng([zlib.crc32(name.encode()), seed]).standard_normal(out[name].shape)
        drawn = base * np.exp(spread * noise) if base else spread * noise
        out[name] = jnp.asarray(drawn.astype(out[name].dtype))
    for name, factor in factors.items():
        out[name] = (out[name] * factor).astype(out[name].dtype)
    return out
```

```python
from contextlib import ExitStack

import numpy as np

import concourse.bass as bass
from concourse import mybir

F32 = mybir.dt.float32
F32R = mybir.dt.float32r
BF16 = mybir.dt.bfloat16
ALU = mybir.AluOpType
ACT = mybir.ActivationFunctionType
AXIS_X = mybir.AxisListType.X

P = 128
BATCH, C, HW, N = 8, 512, 32 * 48, 40
KC = C // P
UNIT = 512
PARTS = HW // UNIT
UNITS = BATCH * PARTS
TILES = UNIT // P
Q = 4
QT = UNIT // Q
BLK = 32
NPAD = 64
HALF = TILES // 2
COPIES = 3
NK = COPIES * N
LAG = 2
EPS = 1e-12


class Step:

    def __init__(self, i, base):
        self.i, self.base = i, base

    def plus(self, n):
        return Step(self.i, self.base + n)

    def times(self, per, plus):
        fixed = per * self.base + plus
        return fixed if self.i is None else self.i * (2 * per) + fixed


def wait(eng, sem, value):
    if isinstance(value, int) and value <= 0:
        return
    eng.wait_ge(sem, value)


def build(nc, x, cent, w, bias, out):
    ctx = ExitStack()
    with ctx:
        def sb(name, shape, dt):
            return ctx.enter_context(nc.sbuf_tensor(name, shape, dt))

        def sem(name):
            return ctx.enter_context(nc.semaphore(name))

        X = [sb(f"x{j}", [P, KC, HW], F32) for j in range(2)]
        XS = [sb(f"xs{j}", [P, C // BLK, QT], F32) for j in range(2)]
        XT = sb("xt", [P, PARTS, TILES, C], F32)
        Z = [sb(f"z{j}", [P, KC, UNIT], F32) for j in range(2)]
        SQ = sb("sq", [P, KC, UNIT], F32)
        YH = [sb(f"yh{j}", [P, KC, UNIT], F32R) for j in range(2)]
        YL = [sb(f"yl{j}", [P, KC, UNIT], F32R) for j in range(2)]
        WH = sb("wh", [P, KC, C], F32R)
        WL = sb("wl", [P, KC, C], F32R)
        OUT = [sb(f"o{j}", [P, KC, UNIT], F32) for j in range(2)]
        alpha = sb("alpha", [P, UNIT], F32)
        simS = sb("sim_s", [P, PARTS, HALF, P], F32)
        oh = sb("oh", [P, PARTS * TILES, NPAD], F32)
        oh3 = sb("oh3", [P, PARTS * TILES, COPIES, N], BF16)
        ohT = [sb(f"oht{j}", [NK, HW], BF16) for j in range(2)]
        sums = sb("sums", [P, C], F32)
        avg = sb("avg", [NK, C], F32)
        rest = sb("rest", [NK, C], F32)
        part1 = sb("part1", [NK, C], BF16)
        part2 = sb("part2", [NK, C], BF16)
        G = sb("g", [NK, C], BF16)
        count = sb("count", [NK, 1], F32)
        count1 = sb("count1", [NK, 1], F32)
        rcount = sb("rcount", [NK, 1], F32)
        best = sb("best", [P, PARTS * TILES], F32)
        tie = sb("tie", [P, PARTS * TILES, N], BF16)
        rank = sb("rank", [P, PARTS * TILES, N], BF16)
        first = sb("first", [P, PARTS * TILES], BF16)
        cnT = sb("cn_t", [P, KC, NPAD], F32)
        bcol = sb("bcol", [P, KC], F32)
        ident = sb("ident", [P, P], F32)
        identb = sb("identb", [P, P], BF16)
        ones = sb("ones", [P, P], F32)
        select = sb("select", [P, COPIES, N], F32)
        weight = sb("weight", [P, N], BF16)
        below2 = sb("below2", [NK, 1], F32)
        below3 = sb("below3", [NK, 1], F32)
        cstat = sb("cstat", [NPAD, 8], F32)
        Wraw = OUT[0]
        craw = SQ[0:NPAD, 0, :]
        cnorm = SQ[0:NPAD, 1, :]
        csq = SQ[0:NPAD, 2, :]

        main = [ctx.enter_context(nc.psum_tensor(f"main{j}", [P, UNIT], F32)) for j in range(2)]
        gat = ctx.enter_context(nc.psum_tensor("gat", [P, 2, UNIT], F32))
        fa = ctx.enter_context(nc.psum_tensor("fa", [P, 2, UNIT], F32))
        fb = ctx.enter_context(nc.psum_tensor("fb", [P, 2, UNIT], F32))
        simP = [fa[:, 0, 0:256], fa[:, 1, 0:256], fa[:, 0, 256:512]]
        simT = fb[:, :, :].rearrange("p a (s h n) -> p (a s h) n", h=2, n=NPAD)
        ohP = fa[:, :, :].rearrange("p a n -> p (a n)").bitcast(BF16)
        sumP, copP = fb[:, 0, :], fb[0:NK, 1, :]

        x_in = [[sem(f"x_in{j}_{u}") for u in range(PARTS)] for j in range(2)]
        xs_in = [sem(f"xs_in{j}") for j in range(2)]
        w_in, c_in, b_in = sem("w_in"), sem("c_in"), sem("b_in")
        out_done = [sem(f"out_done{j}") for j in range(2)]
        const_done, ident_done = sem("const_done"), sem("ident_done")
        craw_done, cstat_done, cn_done, cnT_ps, cnT_done = (
            sem("craw_done"), sem("cstat_done"), sem("cn_done"), sem("cnt_ps"), sem("cnt_done"))
        wT_ps, wh_done, wl_done = sem("wt_ps"), sem("wh_done"), sem("wl_done")
        a_done, simS_done, simT_done = sem("a_done"), sem("sims_done"), sem("simt_done")
        arg_step, oh_done, oh3_done = sem("arg_step"), sem("oh_done"), sem("oh3_done")
        ohP_done, ohT_done = sem("ohp_done"), sem("oht_done")
        tr_done, c_done, sums_done, cop_done = sem("tr_done"), sem("c_done"), sem("sums_done"), sem("cop_done")
        avg_step, g_ready = sem("avg_step"), sem("g_ready")
        gat_done, z_done, sq_done, add_step, s_done = (
            sem("gat_done"), sem("z_done"), sem("sq_done"), sem("add_step"), sem("s_done"))
        one_done, exp_done, za_done, y_done = sem("one_done"), sem("exp_done"), sem("za_done"), sem("y_done")
        hi_done, lo_done, main_done, relu_done = (
            sem("hi_done"), sem("lo_done"), sem("main_done"), sem("relu_done"))

        x_rows = x.rearrange("b (k p) s -> b p k s", p=P)
        x_blocks = x.rearrange("b (m j) s -> b j m s", j=BLK)
        out_rows = out.rearrange("b (k p) s -> b p k s", p=P)
        block = ctx.enter_context(nc.Block())

        def wT(k):
            return (main[0][:, :], main[1][:, :], gat[:, 0, :], gat[:, 1, :])[k]

        def par(b, p=0):
            return (b.base + p) % 2

        def conv_unit(b, p):
            d, q = divmod(p - LAG, PARTS)
            bm = b.plus(d)
            return bm, q, bm.i is not None or 0 <= bm.base < BATCH

        def images(eng, body, lo=1, hi=BATCH - 1):
            for n in range(lo):
                body(Step(None, n))
            pairs = (hi - lo) // 2
            with eng.Fori(0, pairs) as i:
                body(Step(i, lo))
                body(Step(i, lo + 1))
            for n in range(lo + 2 * pairs, BATCH):
                body(Step(None, n))

        def index(b):
            return slice(b.base, b.base + 1) if b.i is None else bass.ds(b.times(1, 0), 1)

        @block.sync
        def _(sp):
            def load_x(b, u):
                wait(sp, y_done, b.times(PARTS, u + 1 - 2 * PARTS))
                sp.dma_start(X[par(b)][:, :, u * UNIT:(u + 1) * UNIT],
                             x_rows[index(b), :, :, u * UNIT:(u + 1) * UNIT].rearrange("b p k s -> (b p) k s")
                             ).then_inc(x_in[par(b)][u], 16)

            def load_xs(b, u):
                wait(sp, tr_done, b.times(PARTS, u - 1))
                for q in range(Q):
                    at = u * UNIT + q * QT
                    sp.dma_start(XS[par(b, u)][q * BLK:(q + 1) * BLK, :, :],
                                 x_blocks[index(b), :, :, at:at + QT].rearrange("b j m s -> (b j) m s")
                                 ).then_inc(xs_in[par(b, u)], 16)

            def store(b, p):
                bm, u, there = conv_unit(b, p)
                if not there:
                    return
                wait(sp, relu_done, b.times(KC * PARTS, KC * (p - LAG + 1)))
                sp.dma_start(out_rows[index(bm), :, :, u * UNIT:(u + 1) * UNIT].rearrange("b p k s -> (b p) k s"),
                             OUT[par(b, p - LAG)][:, :, :]).then_inc(out_done[par(b, p - LAG)], 16)

            def body(b):
                n1, n2 = b.plus(1), b.plus(2)
                has1 = b.i is not None or n1.base < BATCH
                has2 = b.i is not None or n2.base < BATCH
                store(b.plus(-1), PARTS - 1)
                if has1:
                    load_x(n1, 2)
                    load_xs(n1, 2)
                if has2:
                    load_xs(n2, 0)
                store(b, 0)
                if has2:
                    load_x(n2, 0)
                    load_xs(n2, 1)
                store(b, 1)
                if has2:
                    load_x(n2, 1)

            sp.dma_start(craw[0:N, :], cent).then_inc(c_in, 16)
            first_image = Step(None, 0)
            load_x(first_image, 0)
            sp.dma_start(Wraw[:, :, :], w.rearrange("(k p) c -> p k c", p=P)).then_inc(w_in, 16)
            load_x(first_image, 1)
            load_xs(first_image, 0)
            load_x(first_image, 2)
            load_xs(first_image, 1)
            with nc.allow_non_contiguous_dma(reason="512 bias values, once"):
                sp.dma_start(bcol[:, :], bias.rearrange("(k p) -> p k", p=P)).then_inc(b_in, 16)
            load_xs(first_image, 2)
            second = first_image.plus(1)
            load_x(second, 0)
            load_x(second, 1)
            load_xs(second, 0)
            load_xs(second, 1)
            images(sp, body, 1, BATCH - 2)
            end = Step(None, BATCH)
            store(end.plus(-1), PARTS - 1)
            store(end, 0)
            store(end, 1)
            for j in range(2):
                sp.wait_ge(out_done[j], 16 * (UNITS // 2))

        @block.gpsimd
        def _(pool):
            pool.memset(ident[:, :], 0.0).then_inc(ident_done, 1)
            pool.memset(ones[:, :], 1.0).then_inc(const_done, 1)
            pool.memset(select[:, :, :], 0.0).then_inc(ident_done, 1)
            pool.memset(below2[:, :], 0.0).then_inc(ident_done, 1)
            pool.memset(below3[:, :], 0.0).then_inc(ident_done, 1)
            pool.wait_ge(ident_done, 4)
            pool.affine_select(out=ident[:, :], in_=ident[:, :], compare_op=ALU.not_equal, fill=1.0,
                               base=0, pattern=[[-1, P]], channel_multiplier=1).then_inc(ident_done, 1)
            pool.affine_select(out=select[:, :, :], in_=select[:, :, :], compare_op=ALU.not_equal, fill=1.0,
                               base=0, pattern=[[0, COPIES], [-1, N]], channel_multiplier=1).then_inc(ident_done, 1)
            for m, rows in ((below2, N), (below3, 2 * N)):
                pool.affine_select(out=m[:, :], in_=m[:, :], compare_op=ALU.is_gt, fill=-1.0,
                                   base=rows, pattern=[[0, 1]], channel_multiplier=-1).then_inc(const_done, 1)
            pool.wait_ge(ident_done, 6)
            pool.affine_select(out=select[:, :, :], in_=select[:, :, :], compare_op=ALU.not_equal, fill=1.0,
                               base=-NPAD, pattern=[[0, COPIES], [-1, N]], channel_multiplier=1
                               ).then_inc(const_done, 1)
            pool.tensor_copy(identb[:, :], ident[:, :]).then_inc(const_done, 1)

            def y_add(b, p):
                wait(pool, za_done, b.times(PARTS, p + 1))
                z = Z[par(b, p)]
                pool.tensor_tensor(z[:, :, :], z[:, :, :], X[par(b)][:, :, p * UNIT:(p + 1) * UNIT],
                                   ALU.add).then_inc(y_done, 1)

            def body(b):
                for p in range(PARTS):
                    before, q = (b, p - 1) if p else (b.plus(-1), PARTS - 1)
                    if before.i is not None or before.base >= 0:
                        y_add(before, q)
                    wait(pool, sq_done, b.times(2 * PARTS, 2 * p + 2))
                    pool.tensor_tensor(SQ[:, 0:2, :], SQ[:, 0:2, :], SQ[:, 2:4, :], ALU.add).then_inc(add_step, 1)
                    wait(pool, add_step, b.times(PARTS, p + 1))
                    pool.tensor_tensor(SQ[:, 0, :], SQ[:, 0, :], SQ[:, 1, :], ALU.add).then_inc(s_done, 1)

            images(pool, body)
            y_add(Step(None, BATCH - 1), PARTS - 1)

        @block.vector
        def _(dve):
            v_ = nc.vector

            def transpose_unit(b, u):
                wait(dve, xs_in[par(b, u)], unit_loads(b, u))
                wait(dve, c_done, b.times(1, 0))
                v_.transpose(XT[:, u, :, :].rearrange("p t (m j) -> p m t j", j=BLK),
                             XS[par(b, u)][:, :, :]).then_inc(tr_done, 1)

            def unit_loads(b, u):
                fixed = 16 * Q * ((PARTS * b.base + u) // 2 + 1)
                return fixed if b.i is None else b.i * (16 * Q * PARTS) + fixed

            def argmax(b):
                shape = [P, PARTS * TILES, N]
                sims = simT[:, 0:PARTS * TILES, 0:N]
                steps = 4
                wait(dve, simT_done, b.times(1, 1))
                wait(dve, oh_done, b.times(1, 0))
                v_.tensor_reduce(best[:, :], sims, AXIS_X, ALU.max).then_inc(arg_step, 1)
                wait(dve, arg_step, b.times(steps, 1))
                v_.tensor_tensor(tie[:, :, :], sims, best[:, :].unsqueeze(2).to_broadcast(shape),
                                 ALU.is_ge).then_inc(arg_step, 1)
                wait(dve, arg_step, b.times(steps, 2))
                v_.tensor_tensor(rank[:, :, :], tie[:, :, :], weight[:, :].unsqueeze(1).to_broadcast(shape),
                                 ALU.mult).then_inc(arg_step, 1)
                wait(dve, arg_step, b.times(steps, 3))
                v_.tensor_reduce(first[:, :], rank[:, :, :], AXIS_X, ALU.max).then_inc(arg_step, 1)
                wait(dve, arg_step, b.times(steps, 4))
                wait(dve, c_done, b.times(1, 0))
                wait(dve, oh3_done, b.times(1, 0))
                v_.tensor_tensor(oh[:, :, 0:N], rank[:, :, :], first[:, :].unsqueeze(2).to_broadcast(shape),
                                 ALU.is_equal).then_inc(oh_done, 1)

            def averages(b):
                steps = 6
                wait(dve, ohT_done, b.times(1, 1))
                wait(dve, g_ready, b.times(1, 0))
                v_.tensor_scalar(count1[:, :], count[:, :], 1.0, None, ALU.max).then_inc(avg_step, 1)
                wait(dve, avg_step, b.times(steps, 1))
                v_.reciprocal(rcount[:, :], count1[:, :]).then_inc(avg_step, 1)
                wait(dve, avg_step, b.times(steps, 2))
                wait(dve, cop_done, b.times(1, 1))
                v_.tensor_scalar(avg[:, :], copP, rcount[:, :], None, ALU.mult).then_inc(avg_step, 1)
                wait(dve, avg_step, b.times(steps, 3))
                v_.tensor_copy(part1[:, :], avg[:, :]).then_inc(avg_step, 1)
                wait(dve, avg_step, b.times(steps, 4))
                v_.scalar_tensor_tensor(out=rest[:, :], in0=part1[:, :], scalar=below2[:, :], in1=avg[:, :],
                                        op0=ALU.mult, op1=ALU.add).then_inc(avg_step, 1)
                wait(dve, avg_step, b.times(steps, 5))
                v_.tensor_copy(part2[:, :], rest[:, :]).then_inc(avg_step, 1)
                wait(dve, avg_step, b.times(steps, 6))
                wait(dve, gat_done, b.times(KC * PARTS, 0))
                v_.scalar_tensor_tensor(out=G[:, :], in0=part2[:, :], scalar=below3[:, :], in1=rest[:, :],
                                        op0=ALU.mult, op1=ALU.add).then_inc(g_ready, 1)

            def delta(b, p, half):
                wait(dve, gat_done, b.times(KC * PARTS, KC * p + 2 * half + 2))
                wait(dve, hi_done, b.times(PARTS, p - 1))
                wait(dve, lo_done, b.times(PARTS, p - 1))
                k = slice(2 * half, 2 * half + 2)
                v_.tensor_tensor(Z[par(b, p)][:, k, :], gat[:, :, :], X[par(b)][:, k, p * UNIT:(p + 1) * UNIT],
                                 ALU.subtract).then_inc(z_done, 1)

            def scale_delta(b, p):
                z = Z[par(b, p)]
                wait(dve, exp_done, b.times(PARTS, p + 1))
                v_.tensor_tensor(z[:, :, :], z[:, :, :], alpha[:, :].unsqueeze(1).to_broadcast([P, KC, UNIT]),
                                 ALU.mult).then_inc(za_done, 1)

            def low(b, p):
                wait(dve, hi_done, b.times(PARTS, p + 1))
                wait(dve, main_done, b.times(KC * PARTS, KC * (p - 1)))
                j = par(b, p)
                v_.tensor_tensor(YL[j][:, :, :], Z[j][:, :, :], YH[j][:, :, :].bitcast(F32),
                                 ALU.subtract).then_inc(lo_done, 1)

            def body(b):
                nxt = b.plus(1)
                there = b.i is not None or nxt.base < BATCH
                for p in range(PARTS):
                    before, q = (b, p - 1) if p else (b.plus(-1), PARTS - 1)
                    delta(b, p, 0)
                    if there and p == 0:
                        transpose_unit(nxt, 0)
                    if there and p == 1:
                        transpose_unit(nxt, 2)
                    delta(b, p, 1)
                    if there and p == 0:
                        transpose_unit(nxt, 1)
                    if before.i is not None or before.base >= 0:
                        low(before, q)
                    if there and p == 1:
                        argmax(nxt)
                    if there and p == 2:
                        averages(nxt)
                    scale_delta(b, p)

            v_.memset(oh[:, :, :], 0.0).then_inc(const_done, 1)
            for n in range(N):
                last = v_.memset(weight[:, n:n + 1], float(NPAD - n))
            last.then_inc(const_done, 1)
            v_.memset(cnorm, 0.0).then_inc(craw_done, 1)
            dve.wait_ge(cstat_done, 2)
            s = lambda c: cstat[0:N, c:c + 1]
            v_.tensor_scalar(s(2), s(1), EPS, None, ALU.max).then_inc(cstat_done, 1)
            dve.wait_ge(cstat_done, 3)
            v_.reciprocal(s(3), s(2)).then_inc(cstat_done, 1)
            dve.wait_ge(cstat_done, 4)
            v_.scalar_tensor_tensor(out=s(4), in0=s(0), scalar=s(3), in1=s(2),
                                    op0=ALU.mult, op1=ALU.add).then_inc(cstat_done, 1)
            dve.wait_ge(cstat_done, 5)
            v_.tensor_scalar(s(5), s(4), 0.5, EPS, ALU.mult, ALU.max).then_inc(cstat_done, 1)
            dve.wait_ge(cstat_done, 6)
            v_.reciprocal(s(6), s(5)).then_inc(cstat_done, 1)
            dve.wait_ge(cstat_done, 7)
            dve.wait_ge(craw_done, 1)
            v_.tensor_scalar(cnorm[0:N, :], craw[0:N, :], s(6), None, ALU.mult).then_inc(cn_done, 1)
            transpose_unit(Step(None, 0), 0)
            for k in range(KC):
                dve.wait_ge(wh_done, k + 1)
                v_.tensor_tensor(WL[:, k, :], wT(k), WH[:, k, :].bitcast(F32), ALU.subtract).then_inc(wl_done, 1)
            transpose_unit(Step(None, 0), 1)
            transpose_unit(Step(None, 0), 2)
            dve.wait_ge(const_done, 7)
            argmax(Step(None, 0))
            averages(Step(None, 0))
            images(dve, body)
            low(Step(None, BATCH - 1), PARTS - 1)

        @block.scalar
        def _(act):
            a_ = nc.scalar

            def square(b, p, half):
                wait(act, z_done, b.times(2 * PARTS, 2 * p + half + 1))
                wait(act, one_done, b.times(PARTS, p))
                k = slice(2 * half, 2 * half + 2)
                a_.activation(SQ[:, k, :], Z[par(b, p)][:, k, :], ACT.Square).then_inc(sq_done, 1)

            def exp(b, p):
                wait(act, one_done, b.times(PARTS, p + 1))
                wait(act, za_done, b.times(PARTS, p))
                a_.activation(alpha[:, :], gat[:, 0, :], ACT.Exp, scale=-1.0 / C).then_inc(exp_done, 1)

            def high(b, p):
                wait(act, y_done, b.times(PARTS, p + 1))
                wait(act, main_done, b.times(KC * PARTS, KC * (p - 1)))
                a_.activation(YH[par(b, p)][:, :, :], Z[par(b, p)][:, :, :], ACT.Copy).then_inc(hi_done, 1)

            def relu(b, p, o):
                if not conv_unit(b, p)[2]:
                    return
                j = par(b, p - LAG)
                wait(act, main_done, b.times(KC * PARTS, KC * (p - LAG) + o + 1))
                if o == 0:
                    fixed = 16 * ((PARTS * b.base + p - LAG) // 2)
                    wait(act, out_done[j], fixed if b.i is None else b.i * (16 * PARTS) + fixed)
                a_.activation(OUT[j][:, o, :], main[o % 2][:, :], ACT.Relu, bias=bcol[:, o:o + 1]
                              ).then_inc(relu_done, 1)

            def copy_sims(b, u):
                wait(act, a_done, b.times(PARTS, u + 1))
                wait(act, simT_done, b.times(1, 0))
                a_.activation(simS[:, u, :, :].rearrange("p t (q i) -> p q t i", q=Q),
                              simP[u].rearrange("p (q t i) -> p q t i", q=Q, t=HALF), ACT.Copy
                              ).then_inc(simS_done, 1)

            def copy_onehot(b):
                wait(act, oh_done, b.times(1, 1))
                wait(act, ohP_done, b.times(1, 0))
                a_.activation(oh3[:, :, :, :], oh[:, :, 0:N].unsqueeze(2).to_broadcast(
                    [P, PARTS * TILES, COPIES, N]), ACT.Copy).then_inc(oh3_done, 1)

            def evacuate_onehot(b):
                wait(act, ohP_done, b.times(1, 1))
                wait(act, g_ready, b.times(1, 0))
                wait(act, gat_done, b.times(KC * PARTS, -KC * PARTS))
                a_.activation(ohT[par(b)][:, :], ohP[0:NK, 0:HW], ACT.Copy, accum_out=count[:, :]
                              ).then_inc(ohT_done, 1)

            def copy_sums(b):
                wait(act, c_done, b.times(1, 1))
                wait(act, cop_done, b.times(1, 0))
                a_.activation(sums[:, :], sumP, ACT.Copy).then_inc(sums_done, 1)

            def body(b):
                nxt = b.plus(1)
                there = b.i is not None or nxt.base < BATCH
                for p in range(PARTS):
                    before, q = (b, p - 1) if p else (b.plus(-1), PARTS - 1)
                    if before.i is not None or before.base >= 0:
                        relu(before, q, 3)
                    square(b, p, 0)
                    if there and p == 1:
                        copy_sims(nxt, 2)
                    relu(b, p, 0)
                    square(b, p, 1)
                    if there and p == 0:
                        copy_sims(nxt, 0)
                    if there and p == 2:
                        evacuate_onehot(nxt)
                    if before.i is not None or before.base >= 0:
                        high(before, q)
                    relu(b, p, 1)
                    if there and p == 0:
                        copy_sims(nxt, 1)
                    if there and p == 2:
                        copy_sums(nxt)
                    relu(b, p, 2)
                    exp(b, p)
                    if there and p == 1:
                        copy_onehot(nxt)

            act.wait_ge(c_in, 16)
            a_.activation(csq[0:N, :], craw[0:N, :], ACT.Square, accum_out=cstat[0:N, 0:1]).then_inc(cstat_done, 1)
            act.wait_ge(cstat_done, 1)
            a_.activation(cstat[0:N, 1:2], cstat[0:N, 0:1], ACT.Sqrt).then_inc(cstat_done, 1)
            act.wait_ge(cnT_ps, 1)
            a_.activation(cnT[:, :, :], fb[:, 0, 0:KC * NPAD].rearrange("p (k n) -> p k n", k=KC),
                          ACT.Copy).then_inc(cnT_done, 1)
            for k in range(KC):
                act.wait_ge(wT_ps, k + 1)
                a_.activation(WH[:, k, :], wT(k), ACT.Copy).then_inc(wh_done, 1)
            act.wait_ge(b_in, 16)
            b0 = Step(None, 0)
            for u in range(PARTS):
                copy_sims(b0, u)
            copy_onehot(b0)
            evacuate_onehot(b0)
            copy_sums(b0)
            images(act, body, 3)
            end = Step(None, BATCH)
            relu(end.plus(-1), PARTS - 1, 3)
            relu(end, 0, 0)
            high(end.plus(-1), PARTS - 1)
            for o in (1, 2, 3):
                relu(end, 0, o)
            for o in range(KC):
                relu(end, 1, o)

        @block.tensor
        def _(pe):
            t_ = nc.tensor

            def similarities(b, u):
                loaded = 16 * (b.base // 2 + 1)
                wait(pe, x_in[par(b)][u], loaded if b.i is None else b.i * 16 + loaded)
                wait(pe, ohT_done, b.times(1, 0))
                if u == 2:
                    wait(pe, simS_done, b.times(PARTS, 1))
                rows = X[par(b)]
                for k in range(KC):
                    for h in range(2):
                        toks = rows[:, k, u * UNIT:(u + 1) * UNIT].rearrange("p (q s) -> p q s", q=Q)
                        last = t_.matmul(simP[u][NPAD * h:NPAD * (h + 1), :], cnT[:, k, :],
                                         toks[:, :, h * HALF * BLK:(h + 1) * HALF * BLK],
                                         start=(k == 0), stop=(k == KC - 1))
                last.then_inc(a_done, 1)

            def transpose_sims(b):
                wait(pe, simS_done, b.times(PARTS, PARTS))
                wait(pe, g_ready, b.times(1, 0))
                for u in range(PARTS):
                    for t in range(HALF):
                        s = u * HALF + t
                        last = t_.transpose(fb[:, s // 4, (s % 4) * P:(s % 4 + 1) * P], simS[:, u, t, :], ident[:, :])
                last.then_inc(simT_done, 1)

            def slot(u, t):
                return (u * HALF + t % HALF) * 2 + t // HALF

            def transpose_onehot(b):
                wait(pe, oh3_done, b.times(1, 1))
                wait(pe, simS_done, b.times(PARTS, PARTS))
                for u in range(PARTS):
                    for t in range(TILES):
                        dst = ohP[0:NK, u * UNIT:(u + 1) * UNIT].rearrange("n (q t i) -> n q t i", q=Q, t=TILES)
                        last = t_.transpose(dst[:, :, t, :], oh3[:, slot(u, t), :, :].rearrange("p r n -> p (r n)"),
                                            identb[:, :])
                last.then_inc(ohP_done, 1)

            def sum_clusters(b, units):
                if units[0] == 0:
                    wait(pe, oh_done, b.times(1, 1))
                wait(pe, tr_done, b.times(PARTS, units[-1] + 1))
                for u in units:
                    for t in range(HALF):
                        for h in range(2):
                            tile = HALF * h + t
                            last = t_.matmul(sumP[NPAD * h:NPAD * (h + 1), :], oh[:, slot(u, tile), :],
                                             XT[:, u, tile, :], start=(u == 0 and t == 0),
                                             stop=(u == PARTS - 1 and t == HALF - 1))
                if units[-1] == PARTS - 1:
                    last.then_inc(c_done, 1)

            def add_halves(b):
                wait(pe, sums_done, b.times(1, 1))
                t_.matmul(copP, select[:, :, :].rearrange("p r n -> p (r n)"), sums[:, :],
                          start=True, stop=True).then_inc(cop_done, 1)

            def gather(b, p, half):
                wait(pe, g_ready, b.times(1, 1))
                wait(pe, ohT_done, b.times(1, 1))
                if half == 0:
                    wait(pe, exp_done, b.times(PARTS, p))
                    wait(pe, z_done, b.times(2 * PARTS, 2 * p))
                else:
                    wait(pe, z_done, b.times(2 * PARTS, 2 * p + 1))
                for j in range(2):
                    k = 2 * half + j
                    t_.matmul(gat[:, j, :], G[:, k * P:(k + 1) * P], ohT[par(b)][:, p * UNIT:(p + 1) * UNIT],
                              start=True, stop=True).then_inc(gat_done, 1)

            def sum_squares(b, p):
                wait(pe, z_done, b.times(2 * PARTS, 2 * p + 2))
                wait(pe, s_done, b.times(PARTS, p + 1))
                t_.matmul(gat[:, 0, :], ones[:, :], SQ[:, 0, :], start=True, stop=True).then_inc(one_done, 1)

            def convolve(b, p, o):
                if not conv_unit(b, p)[2]:
                    return
                j = par(b, p - LAG)
                if o == 0:
                    wait(pe, hi_done, b.times(PARTS, p - LAG + 1))
                    wait(pe, lo_done, b.times(PARTS, p - LAG + 1))
                wait(pe, relu_done, b.times(KC * PARTS, KC * (p - LAG) + o - 1))
                cols = slice(o * P, (o + 1) * P)
                for k in range(KC):
                    t_.matmul(main[o % 2][:, :], WH[:, k, cols], YH[j][:, k, :], start=(k == 0), stop=False)
                    t_.matmul(main[o % 2][:, :], WH[:, k, cols], YL[j][:, k, :], start=False, stop=False)
                    last = t_.matmul(main[o % 2][:, :], WL[:, k, cols], YH[j][:, k, :], start=False,
                                     stop=(k == KC - 1))
                last.then_inc(main_done, 1)

            def body(b):
                nxt = b.plus(1)
                there = b.i is not None or nxt.base < BATCH
                for p in range(PARTS):
                    gather(b, p, 0)
                    if there and p == 0:
                        similarities(nxt, 0)
                    if there and p == 1:
                        similarities(nxt, 2)
                    if there and p == 2:
                        transpose_onehot(nxt)
                        sum_clusters(nxt, [0])
                    convolve(b, p, 0)
                    gather(b, p, 1)
                    if there and p == 0:
                        similarities(nxt, 1)
                    if there and p == 2:
                        sum_clusters(nxt, [1, 2])
                    convolve(b, p, 1)
                    if there and p == 1:
                        transpose_sims(nxt)
                    convolve(b, p, 2)
                    if there and p == 2:
                        add_halves(nxt)
                    sum_squares(b, p)
                    convolve(b, p, 3)

            pe.wait_ge(const_done, 7)
            pe.wait_ge(ident_done, 6)
            pe.wait_ge(cn_done, 1)
            for k in range(KC):
                last = t_.transpose(fb[:, 0, k * NPAD:(k + 1) * NPAD], cnorm[:, k * P:(k + 1) * P],
                                    ident[0:NPAD, 0:NPAD])
            last.then_inc(cnT_ps, 1)
            pe.wait_ge(w_in, 16)
            for k in range(KC):
                for o in range(KC):
                    last = t_.transpose(wT(k)[:, o * P:(o + 1) * P], Wraw[:, o, k * P:(k + 1) * P], ident[:, :])
                last.then_inc(wT_ps, 1)
            b0 = Step(None, 0)
            pe.wait_ge(cnT_done, 1)
            for u in range(PARTS):
                similarities(b0, u)
            transpose_sims(b0)
            transpose_onehot(b0)
            sum_clusters(b0, [0, 1, 2])
            add_halves(b0)
            pe.wait_ge(wl_done, KC)
            images(pe, body)
            end = Step(None, BATCH)
            for p in range(LAG):
                for o in range(KC):
                    convolve(end, p, o)


def kernel(x, L0_conv_centroids, L0_conv_W, L0_conv_b):
    import concourse.bacc as bacc
    from concourse.bass_utils import run_bass_kernel_spmd

    nc = bacc.Bacc("TRN2", target_bir_lowering=False, num_devices=1)
    x = np.asarray(x)
    shape = x.shape
    arrays = {
        "x": np.ascontiguousarray(x).reshape(BATCH, C, HW),
        "centroids": np.ascontiguousarray(L0_conv_centroids),
        "w": np.ascontiguousarray(L0_conv_W),
        "bias": np.ascontiguousarray(L0_conv_b),
    }
    args = [nc.dram_tensor(n, a.shape, F32, kind="ExternalInput").ap() for n, a in arrays.items()]
    out = nc.dram_tensor("out", (BATCH, C, HW), F32, kind="ExternalOutput").ap()
    build(nc, *args, out)
    got = run_bass_kernel_spmd(nc, [arrays], core_ids=[0])
    return got.results[0]["out"].reshape(shape)
```

```python
from contextlib import ExitStack

import numpy as np

import concourse.bass as bass
from concourse import mybir

F32 = mybir.dt.float32
F32R = mybir.dt.float32r
BF16 = mybir.dt.bfloat16
ALU = mybir.AluOpType
ACT = mybir.ActivationFunctionType
AXIS_X = mybir.AxisListType.X

P = 128
BATCH, C, HW, N = 8, 512, 32 * 48, 40
KC = C // P
UNIT = 512
PARTS = HW // UNIT
UNITS = BATCH * PARTS
TILES = UNIT // P
Q = 4
QT = UNIT // Q
BLK = 32
NPAD = 64
HALF = TILES // 2
COPIES = 3
NK = COPIES * N
LAG = 2
EPS = 1e-12


class Step:

    def __init__(self, i, base):
        self.i, self.base = i, base

    def plus(self, n):
        return Step(self.i, self.base + n)

    def times(self, per, plus):
        fixed = per * self.base + plus
        return fixed if self.i is None else self.i * (2 * per) + fixed


def wait(eng, sem, value):
    if isinstance(value, int) and value <= 0:
        return
    eng.wait_ge(sem, value)


def build(nc, x, cent, w, bias, out):
    ctx = ExitStack()
    with ctx:
        def sb(name, shape, dt):
            return ctx.enter_context(nc.sbuf_tensor(name, shape, dt))

        def sem(name):
            return ctx.enter_context(nc.semaphore(name))

        X = [sb(f"x{j}", [P, KC, HW], F32) for j in range(2)]
        XS = [sb(f"xs{j}", [P, C // BLK, QT], F32) for j in range(2)]
        XT = sb("xt", [P, PARTS, TILES, C], F32)
        Z = [sb(f"z{j}", [P, KC, UNIT], F32) for j in range(2)]
        SQ = sb("sq", [P, KC, UNIT], F32)
        SH = sb("sh", [P, UNIT], F32R)
        SL = sb("sl", [P, UNIT], F32R)
        YH = [sb(f"yh{j}", [P, KC, UNIT], F32R) for j in range(2)]
        YL = [sb(f"yl{j}", [P, KC, UNIT], F32R) for j in range(2)]
        WH = sb("wh", [P, KC, C], F32R)
        WL = sb("wl", [P, KC, C], F32R)
        OUT = [sb(f"o{j}", [P, KC, UNIT], F32) for j in range(2)]
        alpha = sb("alpha", [P, UNIT], F32)
        work = sb("work", [P, 2, C], F32)
        simS = work[:, :, :].rearrange("p a c -> p (a c)")[:, 0:PARTS * HALF * P].rearrange(
            "p (u t s) -> p u t s", u=PARTS, t=HALF)
        avg, rest = work[0:NK, 0, :], work[0:NK, 1, :]
        oh = sb("oh", [P, PARTS * TILES, NPAD], F32)
        oh3 = sb("oh3", [P, PARTS * TILES, COPIES, N], BF16)
        ohT = [sb(f"oht{j}", [NK, HW], BF16) for j in range(2)]
        sumsH = sb("sums_h", [P, C], F32R)
        sumsL = sb("sums_l", [P, C], F32R)
        tie_part = sb("tie_part", [P, C], BF16)
        part = tie_part[0:NK, :]
        tie = tie_part[:, 0:PARTS * TILES * N].rearrange("p (t n) -> p t n", n=N)
        G = sb("g", [NK, C], BF16)
        cols = sb("cols", [P, 6], F32)
        count, count1, rcount = (cols[0:NK, j:j + 1] for j in range(3))
        below2, below3 = cols[0:NK, 3:4], cols[0:NK, 4:5]
        warm = cols[:, 5:6]
        best = sb("best", [P, PARTS * TILES], F32)
        rank = sb("rank", [P, PARTS * TILES, N], BF16)
        first = sb("first", [P, PARTS * TILES], BF16)
        cT = sb("c_t", [P, KC, NPAD], F32)
        bcol = sb("bcol", [P, KC], F32)
        ident = sb("ident", [P, P], F32)
        identb = sb("identb", [P, P], BF16)
        ones = sb("ones", [P, P], F32R)
        select = sb("select", [P, COPIES, N], F32R)
        weight = sb("weight", [P, N], BF16)
        cstat = sb("cstat", [P, 7], F32)
        Wraw = OUT[0]
        select0 = OUT[1][:, 0, 0:NK].rearrange("p (r n) -> p r n", r=COPIES)
        craw, csq = SQ[:, 0, :], SQ[:, 1, :]
        column_tiles = (slice(0, N), slice(NPAD, NPAD + N))

        main = [ctx.enter_context(nc.psum_tensor(f"main{j}", [P, UNIT], F32)) for j in range(2)]
        gat = ctx.enter_context(nc.psum_tensor("gat", [P, 2, UNIT], F32))
        fa = ctx.enter_context(nc.psum_tensor("fa", [P, 2, UNIT], F32))
        fb = ctx.enter_context(nc.psum_tensor("fb", [P, 2, UNIT], F32))
        simP = [fa[:, 0, 0:256], fa[:, 1, 0:256], fa[:, 0, 256:512]]
        simT = fb[:, :, :].rearrange("p a (s h n) -> p (a s h) n", h=2, n=NPAD)
        ohP = fa[:, :, :].rearrange("p a n -> p (a n)").bitcast(BF16)
        sumP, copP = fb[:, 0, :], fb[0:NK, 1, :]

        x_in = [[sem(f"x_in{j}_{u}") for u in range(PARTS)] for j in range(2)]
        xs_in = [sem(f"xs_in{j}") for j in range(2)]
        w_in, c_in, b_in = sem("w_in"), sem("c_in"), sem("b_in")
        out_done = [sem(f"out_done{j}") for j in range(2)]
        warm_done = sem("warm_done")
        const_done, ident_done = sem("const_done"), sem("ident_done")
        cT_ps, cT_done, norm_step = sem("ct_ps"), sem("ct_done"), sem("norm_step")
        wT_ps, wh_done, wl_done = sem("wt_ps"), sem("wh_done"), sem("wl_done")
        a_done, simS_done, simT_done = sem("a_done"), sem("sims_done"), sem("simt_done")
        arg_step, oh_done, oh3_done = sem("arg_step"), sem("oh_done"), sem("oh3_done")
        ohP_done, ohT_done = sem("ohp_done"), sem("oht_done")
        tr_done, c_done, cop_done = sem("tr_done"), sem("c_done"), sem("cop_done")
        sumsH_done, sumsL_done = sem("sumsh_done"), sem("sumsl_done")
        avg_step, g_ready = sem("avg_step"), sem("g_ready")
        gat_done, z_done, sq_done = sem("gat_done"), sem("z_done"), sem("sq_done")
        add01_done, add23_done, s_done, sh_done, sl_done = (
            sem("add01_done"), sem("add23_done"), sem("s_done"), sem("sh_done"), sem("sl_done"))
        y_done = sem("y_done")
        one_done, exp_done, za_done = sem("one_done"), sem("exp_done"), sem("za_done")
        hi_done, lo_done, main_done, relu_done = (
            sem("hi_done"), sem("lo_done"), sem("main_done"), sem("relu_done"))

        x_rows = x.rearrange("b (k p) s -> b p k s", p=P)
        x_blocks = x.rearrange("b (m j) s -> b j m s", j=BLK)
        out_rows = out.rearrange("b (k p) s -> b p k s", p=P)
        block = ctx.enter_context(nc.Block())

        def wT(k):
            return (main[0][:, :], main[1][:, :], fa[:, 0, :], fa[:, 1, :])[k]

        def par(b, p=0):
            return (b.base + p) % 2

        def conv_unit(b, p):
            d, q = divmod(p - LAG, PARTS)
            bm = b.plus(d)
            return bm, q, bm.i is not None or 0 <= bm.base < BATCH

        def sum_bank(b, p):
            return gat[:, 0, :] if conv_unit(b, p)[2] else main[0][:, :]

        def images(eng, body, lo=1, hi=BATCH - 1):
            for n in range(lo):
                body(Step(None, n))
            pairs = (hi - lo) // 2
            with eng.Fori(0, pairs) as i:
                body(Step(i, lo))
                body(Step(i, lo + 1))
            for n in range(lo + 2 * pairs, BATCH):
                body(Step(None, n))

        def index(b):
            return slice(b.base, b.base + 1) if b.i is None else bass.ds(b.times(1, 0), 1)

        @block.sync
        def _(sp):
            def load_x(b, u):
                wait(sp, y_done, b.times(PARTS, u + 1 - 2 * PARTS))
                sp.dma_start(X[par(b)][:, :, u * UNIT:(u + 1) * UNIT],
                             x_rows[index(b), :, :, u * UNIT:(u + 1) * UNIT].rearrange("b p k s -> (b p) k s")
                             ).then_inc(x_in[par(b)][u], 16)

            def load_xs(b, u):
                wait(sp, tr_done, b.times(PARTS, u - 1))
                for q in range(Q):
                    at = u * UNIT + q * QT
                    sp.dma_start(XS[par(b, u)][q * BLK:(q + 1) * BLK, :, :],
                                 x_blocks[index(b), :, :, at:at + QT].rearrange("b j m s -> (b j) m s")
                                 ).then_inc(xs_in[par(b, u)], 16)

            def store(b, p):
                bm, u, there = conv_unit(b, p)
                if not there:
                    return
                wait(sp, relu_done, b.times(KC * PARTS, KC * (p - LAG + 1)))
                sp.dma_start(out_rows[index(bm), :, :, u * UNIT:(u + 1) * UNIT].rearrange("b p k s -> (b p) k s"),
                             OUT[par(b, p - LAG)][:, :, :]).then_inc(out_done[par(b, p - LAG)], 16)

            def body(b):
                n1, n2 = b.plus(1), b.plus(2)
                has1 = b.i is not None or n1.base < BATCH
                has2 = b.i is not None or n2.base < BATCH
                store(b.plus(-1), PARTS - 1)
                if has1:
                    load_x(n1, 2)
                    load_xs(n1, 2)
                if has2:
                    load_xs(n2, 0)
                store(b, 0)
                if has2:
                    load_x(n2, 0)
                    load_xs(n2, 1)
                store(b, 1)
                if has2:
                    load_x(n2, 1)

            for rows in column_tiles:
                sp.dma_start(craw[rows, :], cent).then_inc(c_in, 16)
            first_image = Step(None, 0)
            for u in range(PARTS):
                load_x(first_image, u)
            load_xs(first_image, 0)
            load_xs(first_image, 1)
            load_xs(first_image, 2)
            with nc.allow_non_contiguous_dma(reason="512 bias values, once"):
                sp.dma_start(bcol[:, :], bias.rearrange("(k p) -> p k", p=P)).then_inc(b_in, 16)
            sp.dma_start(Wraw[:, :, :], w.rearrange("(k p) c -> p k c", p=P)).then_inc(w_in, 16)
            second = first_image.plus(1)
            load_x(second, 0)
            load_x(second, 1)
            load_xs(second, 0)
            load_xs(second, 1)
            images(sp, body, 1, BATCH - 2)
            end = Step(None, BATCH)
            store(end.plus(-1), PARTS - 1)
            store(end, 0)
            store(end, 1)
            for j in range(2):
                sp.wait_ge(out_done[j], 16 * (UNITS // 2))

        @block.gpsimd
        def _(pool):
            pool.memset(ident[:, :], 0.0).then_inc(ident_done, 1)
            pool.memset(ones[:, :].bitcast(F32), 1.0).then_inc(const_done, 1)
            pool.memset(select0[:, :, :], 0.0).then_inc(ident_done, 1)
            pool.memset(below2[:, :], 0.0).then_inc(ident_done, 1)
            pool.memset(below3[:, :], 0.0).then_inc(ident_done, 1)
            pool.wait_ge(ident_done, 4)
            pool.affine_select(out=ident[:, :], in_=ident[:, :], compare_op=ALU.not_equal, fill=1.0,
                               base=0, pattern=[[-1, P]], channel_multiplier=1).then_inc(ident_done, 1)
            pool.affine_select(out=select0[:, :, :], in_=select0[:, :, :], compare_op=ALU.not_equal, fill=1.0,
                               base=0, pattern=[[0, COPIES], [-1, N]], channel_multiplier=1).then_inc(ident_done, 1)
            for m, rows in ((below2, N), (below3, 2 * N)):
                pool.affine_select(out=m[:, :], in_=m[:, :], compare_op=ALU.is_gt, fill=-1.0,
                                   base=rows, pattern=[[0, 1]], channel_multiplier=-1).then_inc(const_done, 1)
            pool.wait_ge(ident_done, 6)
            pool.affine_select(out=select0[:, :, :], in_=select0[:, :, :], compare_op=ALU.not_equal, fill=1.0,
                               base=-NPAD, pattern=[[0, COPIES], [-1, N]], channel_multiplier=1
                               ).then_inc(ident_done, 1)
            pool.tensor_copy(identb[:, :], ident[:, :]).then_inc(const_done, 1)
            pool.wait_ge(ident_done, 7)
            pool.tensor_copy(select[:, :, :], select0[:, :, :]).then_inc(const_done, 1)

            def y_add(b, p):
                wait(pool, za_done, b.times(PARTS, p + 1))
                z = Z[par(b, p)][:, :, :]
                pool.tensor_tensor(z, z, X[par(b)][:, :, p * UNIT:(p + 1) * UNIT], ALU.add).then_inc(y_done, 1)

            def body(b):
                for p in range(PARTS):
                    before, q = (b, p - 1) if p else (b.plus(-1), PARTS - 1)
                    wait(pool, sq_done, b.times(2 * PARTS, 2 * p + 1))
                    pool.tensor_tensor(SQ[:, 0, :], SQ[:, 0, :], SQ[:, 1, :], ALU.add).then_inc(add01_done, 1)
                    if before.i is not None or before.base >= 0:
                        y_add(before, q)

            images(pool, body)
            y_add(Step(None, BATCH - 1), PARTS - 1)

        @block.vector
        def _(dve):
            v_ = nc.vector

            def transpose_unit(b, u):
                wait(dve, xs_in[par(b, u)], unit_loads(b, u))
                wait(dve, c_done, b.times(PARTS, u + 1 - PARTS))
                v_.transpose(XT[:, u, :, :].rearrange("p t (m j) -> p m t j", j=BLK),
                             XS[par(b, u)][:, :, :]).then_inc(tr_done, 1)

            def unit_loads(b, u):
                fixed = 16 * Q * ((PARTS * b.base + u) // 2 + 1)
                return fixed if b.i is None else b.i * (16 * Q * PARTS) + fixed

            def argmax(b):
                shape = [P, PARTS * TILES, N]
                sims = simT[:, 0:PARTS * TILES, 0:N]
                steps = 4
                wait(dve, simT_done, b.times(1, 1))
                wait(dve, oh_done, b.times(1, 0))
                v_.tensor_reduce(best[:, :], sims, AXIS_X, ALU.max).then_inc(arg_step, 1)
                wait(dve, arg_step, b.times(steps, 1))
                v_.tensor_tensor(tie[:, :, :], sims, best[:, :].unsqueeze(2).to_broadcast(shape),
                                 ALU.is_ge).then_inc(arg_step, 1)
                wait(dve, arg_step, b.times(steps, 2))
                v_.tensor_tensor(rank[:, :, :], tie[:, :, :], weight[:, :].unsqueeze(1).to_broadcast(shape),
                                 ALU.mult).then_inc(arg_step, 1)
                wait(dve, arg_step, b.times(steps, 3))
                v_.tensor_reduce(first[:, :], rank[:, :, :], AXIS_X, ALU.max).then_inc(arg_step, 1)
                wait(dve, arg_step, b.times(steps, 4))
                wait(dve, c_done, b.times(PARTS, 0))
                wait(dve, oh3_done, b.times(1, 0))
                v_.tensor_tensor(oh[:, :, 0:N], rank[:, :, :], first[:, :].unsqueeze(2).to_broadcast(shape),
                                 ALU.is_equal).then_inc(oh_done, 1)

            AVG_STEPS = 6

            def counts(b):
                wait(dve, ohT_done, b.times(1, 1))
                wait(dve, g_ready, b.times(1, 0))
                v_.tensor_scalar(count1[:, :], count[:, :], 1.0, None, ALU.max).then_inc(avg_step, 1)
                wait(dve, avg_step, b.times(AVG_STEPS, 1))
                v_.reciprocal(rcount[:, :], count1[:, :]).then_inc(avg_step, 1)

            def averages(b):
                steps = AVG_STEPS
                wait(dve, avg_step, b.times(steps, 2))
                wait(dve, cop_done, b.times(1, 1))
                v_.tensor_scalar(avg[:, :], copP, rcount[:, :], None, ALU.mult).then_inc(avg_step, 1)
                wait(dve, avg_step, b.times(steps, 3))
                v_.tensor_copy(part[:, :], avg[:, :]).then_inc(avg_step, 1)
                wait(dve, avg_step, b.times(steps, 4))
                v_.scalar_tensor_tensor(out=rest[:, :], in0=part[:, :], scalar=below2[:, :], in1=avg[:, :],
                                        op0=ALU.mult, op1=ALU.add).then_inc(avg_step, 1)
                wait(dve, avg_step, b.times(steps, 5))
                v_.tensor_copy(part[:, :], rest[:, :]).then_inc(avg_step, 1)
                wait(dve, avg_step, b.times(steps, 6))
                wait(dve, gat_done, b.times(KC * PARTS, 0))
                v_.scalar_tensor_tensor(out=G[:, :], in0=part[:, :], scalar=below3[:, :], in1=rest[:, :],
                                        op0=ALU.mult, op1=ALU.add).then_inc(g_ready, 1)

            def delta(b, p, half):
                wait(dve, gat_done, b.times(KC * PARTS, KC * p + 2 * half + 2))
                wait(dve, hi_done, b.times(PARTS, p - 1))
                wait(dve, lo_done, b.times(PARTS, p - 1))
                k = slice(2 * half, 2 * half + 2)
                v_.tensor_tensor(Z[par(b, p)][:, k, :], gat[:, :, :], X[par(b)][:, k, p * UNIT:(p + 1) * UNIT],
                                 ALU.subtract).then_inc(z_done, 1)

            def scale_delta(b, p):
                z = Z[par(b, p)]
                wait(dve, exp_done, b.times(PARTS, p + 1))
                v_.tensor_tensor(z[:, :, :], z[:, :, :], alpha[:, :].unsqueeze(1).to_broadcast([P, KC, UNIT]),
                                 ALU.mult).then_inc(za_done, 1)

            def add_squares(b, p):
                wait(dve, sq_done, b.times(2 * PARTS, 2 * p + 2))
                v_.tensor_tensor(SQ[:, 2, :], SQ[:, 2, :], SQ[:, 3, :], ALU.add).then_inc(add23_done, 1)
                wait(dve, add23_done, b.times(PARTS, p + 1))
                wait(dve, add01_done, b.times(PARTS, p + 1))
                v_.tensor_tensor(SQ[:, 0, :], SQ[:, 0, :], SQ[:, 2, :], ALU.add).then_inc(s_done, 1)

            def low_sum(b, p):
                wait(dve, sh_done, b.times(PARTS, p + 1))
                wait(dve, one_done, b.times(PARTS, p))
                v_.tensor_tensor(SL[:, :], SQ[:, 0, :], SH[:, :].bitcast(F32), ALU.subtract).then_inc(sl_done, 1)

            def low_clusters(b):
                wait(dve, sumsH_done, b.times(1, 1))
                wait(dve, cop_done, b.times(1, 0))
                v_.tensor_tensor(sumsL[:, :], sumP, sumsH[:, :].bitcast(F32), ALU.subtract).then_inc(sumsL_done, 1)

            def low(b, p):
                wait(dve, hi_done, b.times(PARTS, p + 1))
                wait(dve, main_done, b.times(KC * PARTS, KC * (p - 1)))
                j = par(b, p)
                v_.tensor_tensor(YL[j][:, :, :], Z[j][:, :, :], YH[j][:, :, :].bitcast(F32),
                                 ALU.subtract).then_inc(lo_done, 1)

            def body(b):
                nxt = b.plus(1)
                there = b.i is not None or nxt.base < BATCH
                for p in range(PARTS):
                    before, q = (b, p - 1) if p else (b.plus(-1), PARTS - 1)
                    had = before.i is not None or before.base >= 0
                    delta(b, p, 0)
                    first = b.i is None and b.base == 0
                    alone = not conv_unit(b, p)[2]
                    if first and p == 0:
                        low_weights(1)
                    if had:
                        scale_delta(before, q)
                    if there and p == 0 and not alone:
                        transpose_unit(nxt, 0)
                    if there and p == 2:
                        transpose_unit(nxt, 2)
                    delta(b, p, 1)
                    if first and p == 0:
                        low_weights(2)
                        low_weights(3)
                    add_squares(b, p)
                    low_sum(b, p)
                    if there and p == 0:
                        transpose_unit(nxt, 0 if alone else 1)
                    if alone and had:
                        low(before, q)
                    if there and p == 1:
                        argmax(nxt)
                    if there and p == 1 and alone:
                        transpose_unit(nxt, 1)
                    if there and p == 2:
                        counts(nxt)
                        low_clusters(nxt)
                    if had and not alone:
                        low(before, q)
                    if there and p == 2:
                        averages(nxt)

            def low_weights(k):
                dve.wait_ge(wh_done, k + 1)
                v_.tensor_tensor(WL[:, k, :], wT(k), WH[:, k, :].bitcast(F32), ALU.subtract).then_inc(wl_done, 1)

            v_.memset(cT[:, :, N:NPAD], 0.0).then_inc(cT_done, 1)
            v_.memset(cstat[:, 0:1], 1.0).then_inc(norm_step, 1)
            v_.memset(oh[:, :, :], 0.0).then_inc(const_done, 1)
            for n in range(N):
                last = v_.memset(weight[:, n:n + 1], float(NPAD - n))
            last.then_inc(const_done, 1)
            dve.wait_ge(norm_step, 4)
            s = lambda c: cstat[:, c:c + 1]
            v_.tensor_scalar(s(2), s(1), EPS, None, ALU.max).then_inc(norm_step, 1)
            dve.wait_ge(norm_step, 5)
            v_.reciprocal(s(3), s(2)).then_inc(norm_step, 1)
            dve.wait_ge(norm_step, 6)
            v_.scalar_tensor_tensor(out=s(4), in0=s(0), scalar=s(3), in1=s(2),
                                    op0=ALU.mult, op1=ALU.add).then_inc(norm_step, 1)
            dve.wait_ge(norm_step, 7)
            v_.tensor_scalar(s(5), s(4), 0.5, EPS, ALU.mult, ALU.max).then_inc(norm_step, 1)
            dve.wait_ge(norm_step, 8)
            v_.reciprocal(s(6), s(5)).then_inc(norm_step, 1)
            b0 = Step(None, 0)
            dve.wait_ge(const_done, 7)
            argmax(b0)
            transpose_unit(b0, 0)
            transpose_unit(b0, 1)
            transpose_unit(b0, 2)
            counts(b0)
            low_clusters(b0)
            low_weights(0)
            averages(b0)
            images(dve, body)
            end = Step(None, BATCH - 1)
            scale_delta(end, PARTS - 1)
            low(end, PARTS - 1)

        @block.scalar
        def _(act):
            a_ = nc.scalar

            def square(b, p, half):
                wait(act, z_done, b.times(2 * PARTS, 2 * p + half + 1))
                wait(act, sl_done, b.times(PARTS, p))
                k = slice(2 * half, 2 * half + 2)
                a_.activation(SQ[:, k, :], Z[par(b, p)][:, k, :], ACT.Square).then_inc(sq_done, 1)

            def exp(b, p):
                wait(act, one_done, b.times(PARTS, p + 1))
                wait(act, za_done, b.times(PARTS, p))
                a_.activation(alpha[:, :], sum_bank(b, p), ACT.Exp, scale=-1.0 / C).then_inc(exp_done, 1)

            def high(b, p):
                wait(act, y_done, b.times(PARTS, p + 1))
                wait(act, main_done, b.times(KC * PARTS, KC * (p - 1)))
                a_.activation(YH[par(b, p)][:, :, :], Z[par(b, p)][:, :, :], ACT.Copy).then_inc(hi_done, 1)

            def high_sum(b, p):
                wait(act, s_done, b.times(PARTS, p + 1))
                wait(act, one_done, b.times(PARTS, p))
                a_.activation(SH[:, :], SQ[:, 0, :], ACT.Copy).then_inc(sh_done, 1)

            def relu(b, p, o):
                if not conv_unit(b, p)[2]:
                    return
                j = par(b, p - LAG)
                wait(act, main_done, b.times(KC * PARTS, KC * (p - LAG) + o + 1))
                if o == 0:
                    fixed = 16 * ((PARTS * b.base + p - LAG) // 2)
                    wait(act, out_done[j], fixed if b.i is None else b.i * (16 * PARTS) + fixed)
                a_.activation(OUT[j][:, o, :], main[o % 2][:, :], ACT.Relu, bias=bcol[:, o:o + 1]
                              ).then_inc(relu_done, 1)

            def copy_sims(b, u):
                wait(act, a_done, b.times(PARTS, u + 1))
                wait(act, simT_done, b.times(1, 0))
                wait(act, g_ready, b.times(1, 0))
                a_.activation(simS[:, u, :, :].rearrange("p t (q i) -> p q t i", q=Q),
                              simP[u].rearrange("p (q t i) -> p q t i", q=Q, t=HALF), ACT.Copy,
                              scale=cstat[:, 6:7]).then_inc(simS_done, 1)

            def copy_onehot(b):
                wait(act, oh_done, b.times(1, 1))
                wait(act, ohP_done, b.times(1, 0))
                a_.activation(oh3[:, :, :, :], oh[:, :, 0:N].unsqueeze(2).to_broadcast(
                    [P, PARTS * TILES, COPIES, N]), ACT.Copy).then_inc(oh3_done, 1)

            def evacuate_onehot(b):
                wait(act, ohP_done, b.times(1, 1))
                wait(act, g_ready, b.times(1, 0))
                wait(act, gat_done, b.times(KC * PARTS, -KC * PARTS))
                a_.activation(ohT[par(b)][:, :], ohP[0:NK, 0:HW], ACT.Copy, accum_out=count[:, :]
                              ).then_inc(ohT_done, 1)

            def copy_sums(b):
                wait(act, c_done, b.times(PARTS, PARTS))
                wait(act, cop_done, b.times(1, 0))
                a_.activation(sumsH[:, :], sumP, ACT.Copy).then_inc(sumsH_done, 1)

            def body(b):
                nxt = b.plus(1)
                there = b.i is not None or nxt.base < BATCH
                for p in range(PARTS):
                    before, q = (b, p - 1) if p else (b.plus(-1), PARTS - 1)
                    if before.i is not None or before.base >= 0:
                        relu(before, q, 3)
                    alone = not conv_unit(b, p)[2]
                    square(b, p, 0)
                    if alone and p == 1:
                        copy_sims(nxt, 0)
                    if there and p == 0 and not alone:
                        copy_sims(nxt, 0)
                    relu(b, p, 0)
                    if there and p == 2:
                        evacuate_onehot(nxt)
                    square(b, p, 1)
                    if there and p == (1 if alone else 0):
                        copy_sims(nxt, 1)
                    if there and p == 1 and not alone:
                        copy_sims(nxt, 2)
                    high_sum(b, p)
                    if there and p == 1 and alone:
                        copy_sims(nxt, 2)
                    if there and p == 2:
                        copy_sums(nxt)
                    if before.i is not None or before.base >= 0:
                        high(before, q)
                    relu(b, p, 1)
                    if there and p == 1 and not alone:
                        copy_onehot(nxt)
                    relu(b, p, 2)
                    exp(b, p)
                    if there and p == 1 and alone:
                        copy_onehot(nxt)

            act.wait_ge(norm_step, 1)
            act.wait_ge(c_in, 32)
            for rows in column_tiles:
                a_.activation(csq[rows, :], craw[rows, :], ACT.Square, accum_out=cstat[rows, 0:1]
                              ).then_inc(norm_step, 1)
            act.wait_ge(cT_ps, 1)
            a_.activation(cT[:, :, 0:N], fb[:, 0, 0:KC * N].rearrange("p (k n) -> p k n", k=KC),
                          ACT.Copy).then_inc(cT_done, 1)
            act.wait_ge(norm_step, 3)
            a_.activation(cstat[:, 1:2], cstat[:, 0:1], ACT.Sqrt).then_inc(norm_step, 1)
            act.wait_ge(norm_step, 9)
            a_.activation(warm[:, :], cstat[:, 6:7], ACT.Exp).then_inc(warm_done, 1)
            b0 = Step(None, 0)
            for u in range(PARTS):
                copy_sims(b0, u)
            copy_onehot(b0)
            evacuate_onehot(b0)
            copy_sums(b0)
            for k in range(KC):
                act.wait_ge(wT_ps, k + 1)
                a_.activation(WH[:, k, :], wT(k), ACT.Copy).then_inc(wh_done, 1)
            act.wait_ge(b_in, 16)
            images(act, body, 3)
            end = Step(None, BATCH)
            relu(end.plus(-1), PARTS - 1, 3)
            high(end.plus(-1), PARTS - 1)
            relu(end, 0, 0)
            for o in (1, 2, 3):
                relu(end, 0, o)
            for o in range(KC):
                relu(end, 1, o)

        @block.tensor
        def _(pe):
            t_ = nc.tensor

            def similarities(b, u):
                loaded = 16 * (b.base // 2 + 1)
                wait(pe, x_in[par(b)][u], loaded if b.i is None else b.i * 16 + loaded)
                wait(pe, ohT_done, b.times(1, 0))
                if u == 2:
                    wait(pe, simS_done, b.times(PARTS, 1))
                rows = X[par(b)]
                for k in range(KC):
                    for h in range(2):
                        toks = rows[:, k, u * UNIT:(u + 1) * UNIT].rearrange("p (q s) -> p q s", q=Q)
                        last = t_.matmul(simP[u][NPAD * h:NPAD * (h + 1), :], cT[:, k, :],
                                         toks[:, :, h * HALF * BLK:(h + 1) * HALF * BLK],
                                         start=(k == 0), stop=(k == KC - 1))
                last.then_inc(a_done, 1)

            def transpose_sims(b):
                wait(pe, simS_done, b.times(PARTS, PARTS))
                wait(pe, g_ready, b.times(1, 0))
                for u in range(PARTS):
                    for t in range(HALF):
                        s = u * HALF + t
                        last = t_.transpose(fb[:, s // 4, (s % 4) * P:(s % 4 + 1) * P], simS[:, u, t, :], ident[:, :])
                last.then_inc(simT_done, 1)

            def slot(u, t):
                return (u * HALF + t % HALF) * 2 + t // HALF

            def transpose_onehot(b):
                wait(pe, oh3_done, b.times(1, 1))
                wait(pe, simS_done, b.times(PARTS, PARTS))
                for u in range(PARTS):
                    for t in range(TILES):
                        dst = ohP[0:NK, u * UNIT:(u + 1) * UNIT].rearrange("n (q t i) -> n q t i", q=Q, t=TILES)
                        last = t_.transpose(dst[:, :, t, :], oh3[:, slot(u, t), :, :].rearrange("p r n -> p (r n)"),
                                            identb[:, :])
                last.then_inc(ohP_done, 1)

            def sum_clusters(b, units):
                if units[0] == 0:
                    wait(pe, oh_done, b.times(1, 1))
                for u in units:
                    wait(pe, tr_done, b.times(PARTS, u + 1))
                    for t in range(HALF):
                        for h in range(2):
                            tile = HALF * h + t
                            last = t_.matmul(sumP[NPAD * h:NPAD * (h + 1), :], oh[:, slot(u, tile), :],
                                             XT[:, u, tile, :], start=(u == 0 and t == 0),
                                             stop=(u == PARTS - 1 and t == HALF - 1))
                    last.then_inc(c_done, 1)

            def add_halves(b):
                wait(pe, sumsH_done, b.times(1, 1))
                wait(pe, sumsL_done, b.times(1, 1))
                rows = select[:, :, :].rearrange("p r n -> p (r n)")
                t_.matmul(copP, rows, sumsH[:, :], start=True, stop=False)
                t_.matmul(copP, rows, sumsL[:, :], start=False, stop=True).then_inc(cop_done, 1)

            def gather(b, p, half):
                wait(pe, g_ready, b.times(1, 1))
                wait(pe, ohT_done, b.times(1, 1))
                if half == 0:
                    if conv_unit(b, p)[2]:
                        wait(pe, exp_done, b.times(PARTS, p))
                    wait(pe, z_done, b.times(2 * PARTS, 2 * p))
                else:
                    wait(pe, z_done, b.times(2 * PARTS, 2 * p + 1))
                for j in range(2):
                    k = 2 * half + j
                    t_.matmul(gat[:, j, :], G[:, k * P:(k + 1) * P], ohT[par(b)][:, p * UNIT:(p + 1) * UNIT],
                              start=True, stop=True).then_inc(gat_done, 1)

            def sum_squares(b, p):
                wait(pe, z_done, b.times(2 * PARTS, 2 * p + 2))
                wait(pe, sh_done, b.times(PARTS, p + 1))
                wait(pe, sl_done, b.times(PARTS, p + 1))
                if not conv_unit(b, p)[2]:
                    wait(pe, exp_done, b.times(PARTS, p))
                t_.matmul(sum_bank(b, p), ones[:, :], SH[:, :], start=True, stop=False)
                t_.matmul(sum_bank(b, p), ones[:, :], SL[:, :], start=False, stop=True).then_inc(one_done, 1)

            def convolve(b, p, o):
                if not conv_unit(b, p)[2]:
                    return
                j = par(b, p - LAG)
                if o == 0:
                    wait(pe, hi_done, b.times(PARTS, p - LAG + 1))
                    wait(pe, lo_done, b.times(PARTS, p - LAG + 1))
                wait(pe, relu_done, b.times(KC * PARTS, KC * (p - LAG) + o - 1))
                cols = slice(o * P, (o + 1) * P)
                for k in range(KC):
                    t_.matmul(main[o % 2][:, :], WH[:, k, cols], YH[j][:, k, :], start=(k == 0), stop=False)
                    t_.matmul(main[o % 2][:, :], WH[:, k, cols], YL[j][:, k, :], start=False, stop=False)
                    last = t_.matmul(main[o % 2][:, :], WL[:, k, cols], YH[j][:, k, :], start=False,
                                     stop=(k == KC - 1))
                last.then_inc(main_done, 1)

            def body(b):
                nxt = b.plus(1)
                there = b.i is not None or nxt.base < BATCH
                for p in range(PARTS):
                    alone = not conv_unit(b, p)[2]
                    gather(b, p, 0)
                    if alone:
                        gather(b, p, 1)
                        if p == 0:
                            pe.wait_ge(wl_done, KC)
                    if there and p == 0:
                        similarities(nxt, 0)
                    convolve(b, p, 0)
                    if not alone:
                        gather(b, p, 1)
                    if there and p == (1 if alone else 0):
                        similarities(nxt, 1)
                    if there and p == 1:
                        similarities(nxt, 2)
                    if there and p == 2:
                        transpose_onehot(nxt)
                        sum_clusters(nxt, range(PARTS))
                    convolve(b, p, 1)
                    if there and p == 1:
                        transpose_sims(nxt)
                    if there and p == 2:
                        add_halves(nxt)
                    convolve(b, p, 2)
                    sum_squares(b, p)
                    convolve(b, p, 3)

            pe.wait_ge(ident_done, 5)
            pe.wait_ge(c_in, 32)
            for k in range(KC):
                last = t_.transpose(fb[:, 0, k * N:(k + 1) * N], craw[0:N, k * P:(k + 1) * P], ident[0:N, 0:N])
            last.then_inc(cT_ps, 1)
            b0 = Step(None, 0)
            pe.wait_ge(cT_done, 2)
            for u in range(PARTS):
                similarities(b0, u)
            transpose_sims(b0)
            pe.wait_ge(const_done, 7)
            sum_clusters(b0, [0])
            transpose_onehot(b0)
            sum_clusters(b0, [1, 2])
            pe.wait_ge(w_in, 16)
            pe.wait_ge(ohT_done, 1)
            for k in range(KC):
                if k == HALF:
                    add_halves(b0)
                for o in range(KC):
                    last = t_.transpose(wT(k)[:, o * P:(o + 1) * P], Wraw[:, o, k * P:(k + 1) * P], ident[:, :])
                last.then_inc(wT_ps, 1)
            images(pe, body)
            end = Step(None, BATCH)
            for p in range(LAG):
                for o in range(KC):
                    convolve(end, p, o)


def kernel(x, L0_conv_centroids, L0_conv_W, L0_conv_b):
    import concourse.bacc as bacc
    from concourse.bass_utils import run_bass_kernel_spmd

    nc = bacc.Bacc("TRN2", target_bir_lowering=False, num_devices=1)
    x = np.asarray(x)
    shape = x.shape
    arrays = {
        "x": np.ascontiguousarray(x).reshape(BATCH, C, HW),
        "centroids": np.ascontiguousarray(L0_conv_centroids),
        "w": np.ascontiguousarray(L0_conv_W),
        "bias": np.ascontiguousarray(L0_conv_b),
    }
    args = [nc.dram_tensor(n, a.shape, F32, kind="ExternalInput").ap() for n, a in arrays.items()]
    out = nc.dram_tensor("out", (BATCH, C, HW), F32, kind="ExternalOutput").ap()
    build(nc, *args, out)
    got = run_bass_kernel_spmd(nc, [arrays], core_ids=[0])
    return got.results[0]["out"].reshape(shape)
```

```python
from contextlib import ExitStack

import numpy as np

import concourse.bass as bass
from concourse import mybir

F32 = mybir.dt.float32
F32R = mybir.dt.float32r
BF16 = mybir.dt.bfloat16
ALU = mybir.AluOpType
ACT = mybir.ActivationFunctionType
AXIS_X = mybir.AxisListType.X

P = 128
BATCH, C, HW, N = 8, 512, 32 * 48, 40
KC = C // P
UNIT = 512
PARTS = HW // UNIT
UNITS = BATCH * PARTS
TILES = UNIT // P
Q = 4
QT = UNIT // Q
BLK = 32
NPAD = 64
HALF = TILES // 2
COPIES = 3
NK = COPIES * N
HALF_K = KC // 2
LAG = 2
EPS = 1e-12


class Step:

    def __init__(self, i, base):
        self.i, self.base = i, base

    def plus(self, n):
        return Step(self.i, self.base + n)

    def times(self, per, plus):
        fixed = per * self.base + plus
        return fixed if self.i is None else self.i * (2 * per) + fixed


def wait(eng, sem, value):
    if isinstance(value, int) and value <= 0:
        return
    eng.wait_ge(sem, value)


def build(nc, x, cent, w, bias, out):
    ctx = ExitStack()
    with ctx:
        def sb(name, shape, dt):
            return ctx.enter_context(nc.sbuf_tensor(name, shape, dt))

        def sem(name):
            return ctx.enter_context(nc.semaphore(name))

        X = [sb(f"x{j}", [P, KC, HW], F32) for j in range(2)]
        XS = [sb(f"xs{j}", [P, C // BLK, QT], F32) for j in range(2)]
        XT = sb("xt", [P, PARTS, TILES, C], F32)
        Z = [sb(f"z{j}", [P, KC, UNIT], F32) for j in range(2)]
        SQ = sb("sq", [P, KC, UNIT], F32)
        SH = sb("sh", [P, UNIT], F32R)
        SL = sb("sl", [P, UNIT], F32R)
        YH = [sb(f"yh{j}", [P, KC, UNIT], F32R) for j in range(2)]
        YL = [sb(f"yl{j}", [P, KC, UNIT], F32R) for j in range(2)]
        WH = sb("wh", [P, KC, C], F32R)
        WL = sb("wl", [P, KC, C], F32R)
        OUT = [sb(f"o{j}", [P, KC, UNIT], F32) for j in range(2)]
        alpha = sb("alpha", [P, UNIT], F32)
        work = sb("work", [P, 2, C], F32)
        simS = work[:, :, :].rearrange("p a c -> p (a c)")[:, 0:PARTS * HALF * P].rearrange(
            "p (u t s) -> p u t s", u=PARTS, t=HALF)
        avg, rest = work[0:NK, 0, :], work[0:NK, 1, :]
        oh = sb("oh", [P, PARTS * TILES, NPAD], F32)
        oh3 = sb("oh3", [P, PARTS * TILES, COPIES, N], BF16)
        ohT = [sb(f"oht{j}", [NK, HW], BF16) for j in range(2)]
        sumsH = sb("sums_h", [P, C], F32R)
        sumsL = sb("sums_l", [P, C], F32R)
        tie_part = sb("tie_part", [P, C], BF16)
        part = tie_part[0:NK, :]
        tie = tie_part[:, 0:PARTS * TILES * N].rearrange("p (t n) -> p t n", n=N)
        G = sb("g", [NK, C], BF16)
        cols = sb("cols", [P, 6], F32)
        count, count1, rcount = (cols[0:NK, j:j + 1] for j in range(3))
        below2, below3 = cols[0:NK, 3:4], cols[0:NK, 4:5]
        warm = cols[:, 5:6]
        best = sb("best", [P, PARTS * TILES], F32)
        rank = sb("rank", [P, PARTS * TILES, N], BF16)
        first = sb("first", [P, PARTS * TILES], BF16)
        cT = sb("c_t", [P, KC, NPAD], F32)
        bcol = sb("bcol", [P, KC], F32)
        ident = sb("ident", [P, P], F32)
        identb = sb("identb", [P, P], BF16)
        ones = sb("ones", [P, P], F32R)
        select = sb("select", [P, COPIES, N], F32R)
        weight = sb("weight", [P, N], BF16)
        cstat = sb("cstat", [P, 7], F32)
        Wraw = OUT[0]
        select0 = OUT[1][:, 0, 0:NK].rearrange("p (r n) -> p r n", r=COPIES)
        craw, csq = SQ[:, 0, :], SQ[:, 1, :]
        column_tiles = (slice(0, N), slice(NPAD, NPAD + N))

        main = ctx.enter_context(nc.psum_tensor("main", [P, 2, UNIT], F32))
        gat = ctx.enter_context(nc.psum_tensor("gat", [P, 2, UNIT], F32))
        fa = ctx.enter_context(nc.psum_tensor("fa", [P, 2, UNIT], F32))
        fb = ctx.enter_context(nc.psum_tensor("fb", [P, 2, UNIT], F32))
        simP = [fa[:, 0, 0:256], fa[:, 1, 0:256], fa[:, 0, 256:512]]
        simT = fb[:, :, :].rearrange("p a (s h n) -> p (a s h) n", h=2, n=NPAD)
        ohP = fa[:, :, :].rearrange("p a n -> p (a n)").bitcast(BF16)
        sumP, copP = fb[:, 0, :], fb[0:NK, 1, :]

        x_in = [[sem(f"x_in{j}_{u}") for u in range(PARTS)] for j in range(2)]
        xs_in = [sem(f"xs_in{j}") for j in range(2)]
        xs2_in = sem("xs2_in")
        w_in, b_in = sem("w_in"), sem("b_in")
        c_in = [sem(f"c_in{j}") for j in range(2)]
        out_done = [sem(f"out_done{j}") for j in range(2)]
        warm_done = sem("warm_done")
        const_done, ident_done = sem("const_done"), sem("ident_done")
        cT_ps, cT_done, norm_step = sem("ct_ps"), sem("ct_done"), sem("norm_step")
        wT_ps, wh_done, wl_done = sem("wt_ps"), sem("wh_done"), sem("wl_done")
        a_done, simS_done, simT_done = sem("a_done"), sem("sims_done"), sem("simt_done")
        arg_step, oh_done, oh3_done = sem("arg_step"), sem("oh_done"), sem("oh3_done")
        ohP_done, ohT_done = sem("ohp_done"), sem("oht_done")
        tr_done, c_done, cop_done = sem("tr_done"), sem("c_done"), sem("cop_done")
        sumsH_done, sumsL_done = sem("sumsh_done"), sem("sumsl_done")
        avg_step, g_ready = sem("avg_step"), sem("g_ready")
        gat_done, z_done, sq_done = sem("gat_done"), sem("z_done"), sem("sq_done")
        add01_done, add23_done, s_done, sh_done, sl_done = (
            sem("add01_done"), sem("add23_done"), sem("s_done"), sem("sh_done"), sem("sl_done"))
        y_done = sem("y_done")
        za_half, hi_half, lo_half = sem("za_half"), sem("hi_half"), sem("lo_half")
        y_half = sem("y_half")
        one_done, exp_done, za_done = sem("one_done"), sem("exp_done"), sem("za_done")
        hi_done, lo_done, main_done, relu_done = (
            sem("hi_done"), sem("lo_done"), sem("main_done"), sem("relu_done"))

        x_rows = x.rearrange("b (k p) s -> b p k s", p=P)
        x_blocks = x.rearrange("b (m j) s -> b j m s", j=BLK)
        out_rows = out.rearrange("b (k p) s -> b p k s", p=P)
        block = ctx.enter_context(nc.Block())

        def wT(k):
            return (main[:, 0, :], main[:, 1, :], gat[:, 0, :], gat[:, 1, :])[k]

        def par(b, p=0):
            return (b.base + p) % 2

        def previous(b, p):
            return (b, p - 1) if p else (b.plus(-1), PARTS - 1)

        def conv_unit(b, p):
            d, q = divmod(p - LAG, PARTS)
            bm = b.plus(d)
            return bm, q, bm.i is not None or 0 <= bm.base < BATCH

        def sum_bank(b, p):
            v = None if b.i is not None else PARTS * b.base + p
            if v == 0:
                return main[:, 0, :], False
            if v == 1 or (b.i is None and b.base == BATCH - 1):
                return fa[:, 0, :], False
            return gat[:, 0, :], True

        def y_shares(b, p):
            n = PARTS * b.base + p - (UNITS - 1 - PARTS)
            return None if b.i is not None or n < 0 else n + 2

        def gather_banks(b, p, half):
            return main if b.i is None and (b.base, p, half) == (0, 0, 1) else gat

        def xs_of(b, u):
            if b.i is None and (b.base, u) == (0, 2):
                return Z[1][:, :, :].rearrange("p k (m i) -> p (k m) i", i=QT), xs2_in, 16 * Q
            j = par(b, u)
            early = j == 1 or (b.i is None and (b.base, u) == (0, 0))
            fixed = 16 * Q * ((PARTS * b.base + u) // 2 + early)
            return XS[j], xs_in[j], fixed if b.i is None else b.i * (16 * Q * PARTS) + fixed

        def images(eng, body, lo=1, hi=BATCH - 1):
            for n in range(1, lo):
                body(Step(None, n))
            pairs = (hi - lo) // 2
            with eng.Fori(0, pairs) as i:
                body(Step(i, lo))
                body(Step(i, lo + 1))
            for n in range(lo + 2 * pairs, BATCH):
                body(Step(None, n))

        def index(b):
            return slice(b.base, b.base + 1) if b.i is None else bass.ds(b.times(1, 0), 1)

        @block.sync
        def _(sp):
            def load_x(b, u):
                wait(sp, y_done, b.times(PARTS, u + 1 - 2 * PARTS))
                if b.i is None and (b.base, u) == (2, 0):
                    sp.wait_ge(y_half, 1)
                sp.dma_start(X[par(b)][:, :, u * UNIT:(u + 1) * UNIT],
                             x_rows[index(b), :, :, u * UNIT:(u + 1) * UNIT].rearrange("b p k s -> (b p) k s")
                             ).then_inc(x_in[par(b)][u], 16)

            def load_xs(b, u):
                dst, sem, _ = xs_of(b, u)
                if sem is not xs2_in:
                    wait(sp, tr_done, b.times(PARTS, u - 1))
                for q in range(Q):
                    at = u * UNIT + q * QT
                    sp.dma_start(dst[q * BLK:(q + 1) * BLK, :, :],
                                 x_blocks[index(b), :, :, at:at + QT].rearrange("b j m s -> (b j) m s")
                                 ).then_inc(sem, 16)

            def store(b, p):
                bm, u, there = conv_unit(b, p)
                if not there:
                    return
                wait(sp, relu_done, b.times(KC * PARTS, KC * (p - LAG + 1)))
                sp.dma_start(out_rows[index(bm), :, :, u * UNIT:(u + 1) * UNIT].rearrange("b p k s -> (b p) k s"),
                             OUT[par(b, p - LAG)][:, :, :]).then_inc(out_done[par(b, p - LAG)], 16)

            def body(b):
                n1, n2 = b.plus(1), b.plus(2)
                has1 = b.i is not None or n1.base < BATCH
                has2 = b.i is not None or n2.base < BATCH
                store(b.plus(-1), PARTS - 1)
                if has1:
                    load_x(n1, 2)
                    load_xs(n1, 2)
                if has2:
                    load_xs(n2, 0)
                store(b, 0)
                if has2:
                    load_x(n2, 0)
                    load_xs(n2, 1)
                store(b, 1)
                if has2:
                    load_x(n2, 1)

            sp.dma_start(craw[column_tiles[0], :], cent).then_inc(c_in[0], 16)
            first_image = Step(None, 0)
            for u in range(PARTS):
                load_x(first_image, u)
                if u == 0:
                    sp.dma_start(craw[column_tiles[1], :], cent).then_inc(c_in[1], 16)
            load_xs(first_image, 0)
            sp.dma_start(Wraw[:, :, :], w.rearrange("(k p) c -> p k c", p=P)).then_inc(w_in, 16)
            load_xs(first_image, 1)
            load_xs(first_image, 2)
            with nc.allow_non_contiguous_dma(reason="512 bias values, once"):
                sp.dma_start(bcol[:, :], bias.rearrange("(k p) -> p k", p=P)).then_inc(b_in, 16)
            second = first_image.plus(1)
            load_x(second, 0)
            load_xs(second, 0)
            load_x(second, 1)
            load_x(second, 2)
            load_xs(second, 1)
            load_xs(second, 2)
            third = first_image.plus(2)
            load_xs(third, 0)
            load_x(third, 0)
            load_xs(third, 1)
            load_x(third, 1)
            images(sp, body, 1, BATCH - 2)
            end = Step(None, BATCH)
            store(end.plus(-1), PARTS - 1)
            store(end, 0)
            last, at, j = BATCH - 1, (PARTS - 1) * UNIT, (UNITS - 1) % 2
            for o in range(KC):
                sp.wait_ge(relu_done, KC * (UNITS - 1) + o + 1)
                sp.dma_start(out[last, o * P:(o + 1) * P, at:at + UNIT], OUT[j][:, o, :]).then_inc(out_done[j], 16)
            sp.wait_ge(out_done[1 - j], 16 * (UNITS // 2))
            sp.wait_ge(out_done[j], 16 * (UNITS // 2 - 1 + KC))

        @block.gpsimd
        def _(pool):
            pool.memset(ident[:, :], 0.0).then_inc(ident_done, 1)
            pool.memset(ones[:, :].bitcast(F32), 1.0).then_inc(const_done, 1)
            pool.memset(select0[:, :, :], 0.0).then_inc(ident_done, 1)
            pool.memset(below2[:, :], 0.0).then_inc(ident_done, 1)
            pool.memset(below3[:, :], 0.0).then_inc(ident_done, 1)
            pool.wait_ge(ident_done, 4)
            pool.affine_select(out=ident[:, :], in_=ident[:, :], compare_op=ALU.not_equal, fill=1.0,
                               base=0, pattern=[[-1, P]], channel_multiplier=1).then_inc(ident_done, 1)
            pool.affine_select(out=select0[:, :, :], in_=select0[:, :, :], compare_op=ALU.not_equal, fill=1.0,
                               base=0, pattern=[[0, COPIES], [-1, N]], channel_multiplier=1).then_inc(ident_done, 1)
            for m, rows in ((below2, N), (below3, 2 * N)):
                pool.affine_select(out=m[:, :], in_=m[:, :], compare_op=ALU.is_gt, fill=-1.0,
                                   base=rows, pattern=[[0, 1]], channel_multiplier=-1).then_inc(const_done, 1)
            pool.wait_ge(ident_done, 6)
            pool.affine_select(out=select0[:, :, :], in_=select0[:, :, :], compare_op=ALU.not_equal, fill=1.0,
                               base=-NPAD, pattern=[[0, COPIES], [-1, N]], channel_multiplier=1
                               ).then_inc(ident_done, 1)
            pool.tensor_copy(identb[:, :], ident[:, :]).then_inc(const_done, 1)
            pool.wait_ge(ident_done, 7)
            pool.tensor_copy(select[:, :, :], select0[:, :, :]).then_inc(const_done, 1)

            def y_add(b, p):
                chunks = KC if y_shares(b, p) is None else HALF_K
                wait(pool, za_done, b.times(PARTS, p + 1))
                z = Z[par(b, p)][:, 0:chunks, :]
                pool.tensor_tensor(z, z, X[par(b)][:, 0:chunks, p * UNIT:(p + 1) * UNIT], ALU.add).then_inc(y_done, 1)

            def add01(b, p):
                wait(pool, sq_done, b.times(2 * PARTS, 2 * p + 1))
                pool.tensor_tensor(SQ[:, 0, :], SQ[:, 0, :], SQ[:, 1, :], ALU.add).then_inc(add01_done, 1)

            def low(b, p):
                wait(pool, hi_done, b.times(PARTS, p + 1))
                wait(pool, main_done, b.times(KC * PARTS, KC * (p - 1)))
                j = par(b, p)
                pool.tensor_tensor(YL[j][:, :, :], Z[j][:, :, :], YH[j][:, :, :].bitcast(F32),
                                   ALU.subtract).then_inc(lo_done, 1)

            def body(b):
                for p in range(PARTS):
                    before, q = previous(b, p)
                    add01(b, p)
                    y_add(before, q)
                    if p == PARTS - 1 and (b.i is not None or b.base < BATCH - 1):
                        low(before, q)

            b0 = Step(None, 0)
            z, upper = Z[0], slice(HALF_K, KC)
            add01(b0, 0)
            add01(b0, 1)
            pool.wait_ge(za_done, 1)
            pool.tensor_tensor(z[:, upper, :], z[:, upper, :], X[0][:, upper, 0:UNIT], ALU.add).then_inc(y_done, 1)
            pool.wait_ge(hi_done, 1)
            pool.tensor_tensor(YL[0][:, upper, :], z[:, upper, :], YH[0][:, upper, :].bitcast(F32), ALU.subtract
                               ).then_inc(lo_done, 1)
            pool.wait_ge(exp_done, 2)
            z = Z[1][:, :, :]
            pool.tensor_tensor(z, z, alpha[:, :].unsqueeze(1).to_broadcast([P, KC, UNIT]), ALU.mult
                               ).then_inc(za_done, 1)
            add01(b0, 2)
            y_add(b0, 1)
            low(b0, 1)
            images(pool, body)
            y_add(Step(None, BATCH - 1), PARTS - 1)

        @block.vector
        def _(dve):
            v_ = nc.vector

            def transpose_unit(b, u, halves=(0, 1)):
                src, sem, landed = xs_of(b, u)
                M = C // BLK
                blocks = slice(halves[0] * M // 2, (halves[-1] + 1) * M // 2)
                if halves[0] == 0:
                    wait(dve, sem, landed)
                    wait(dve, c_done, b.times(PARTS, u + 1 - PARTS))
                last = v_.transpose(XT[:, u, :, :].rearrange("p t (m j) -> p m t j", j=BLK)[:, blocks, :, :],
                                    src[:, blocks, :])
                if halves[-1] == 1:
                    last.then_inc(tr_done, 1)

            def argmax(b):
                shape = [P, PARTS * TILES, N]
                sims = simT[:, 0:PARTS * TILES, 0:N]
                steps = 4
                wait(dve, simT_done, b.times(1, 1))
                wait(dve, oh_done, b.times(1, 0))
                v_.tensor_reduce(best[:, :], sims, AXIS_X, ALU.max).then_inc(arg_step, 1)
                wait(dve, arg_step, b.times(steps, 1))
                v_.tensor_tensor(tie[:, :, :], sims, best[:, :].unsqueeze(2).to_broadcast(shape),
                                 ALU.is_ge).then_inc(arg_step, 1)
                wait(dve, arg_step, b.times(steps, 2))
                v_.tensor_tensor(rank[:, :, :], tie[:, :, :], weight[:, :].unsqueeze(1).to_broadcast(shape),
                                 ALU.mult).then_inc(arg_step, 1)
                wait(dve, arg_step, b.times(steps, 3))
                v_.tensor_reduce(first[:, :], rank[:, :, :], AXIS_X, ALU.max).then_inc(arg_step, 1)
                wait(dve, arg_step, b.times(steps, 4))
                wait(dve, c_done, b.times(PARTS, 0))
                wait(dve, oh3_done, b.times(1, 0))
                v_.tensor_tensor(oh[:, :, 0:N], rank[:, :, :], first[:, :].unsqueeze(2).to_broadcast(shape),
                                 ALU.is_equal).then_inc(oh_done, 1)

            AVG_STEPS = 6

            def counts(b):
                wait(dve, ohT_done, b.times(1, 1))
                wait(dve, g_ready, b.times(1, 0))
                v_.tensor_scalar(count1[:, :], count[:, :], 1.0, None, ALU.max).then_inc(avg_step, 1)
                wait(dve, avg_step, b.times(AVG_STEPS, 1))
                v_.reciprocal(rcount[:, :], count1[:, :]).then_inc(avg_step, 1)

            def averages(b):
                steps = AVG_STEPS
                wait(dve, avg_step, b.times(steps, 2))
                wait(dve, cop_done, b.times(1, 1))
                v_.tensor_scalar(avg[:, :], copP, rcount[:, :], None, ALU.mult).then_inc(avg_step, 1)
                wait(dve, avg_step, b.times(steps, 3))
                v_.tensor_copy(part[:, :], avg[:, :]).then_inc(avg_step, 1)
                wait(dve, avg_step, b.times(steps, 4))
                v_.scalar_tensor_tensor(out=rest[:, :], in0=part[:, :], scalar=below2[:, :], in1=avg[:, :],
                                        op0=ALU.mult, op1=ALU.add).then_inc(avg_step, 1)
                wait(dve, avg_step, b.times(steps, 5))
                v_.tensor_copy(part[:, :], rest[:, :]).then_inc(avg_step, 1)
                wait(dve, avg_step, b.times(steps, 6))
                wait(dve, gat_done, b.times(KC * PARTS, 0))
                v_.scalar_tensor_tensor(out=G[:, :], in0=part[:, :], scalar=below3[:, :], in1=rest[:, :],
                                        op0=ALU.mult, op1=ALU.add).then_inc(g_ready, 1)

            def delta(b, p, half):
                wait(dve, gat_done, b.times(KC * PARTS, KC * p + 2 * half + 2))
                wait(dve, hi_done, b.times(PARTS, p - 1))
                wait(dve, lo_done, b.times(PARTS, p - 1))
                k = slice(2 * half, 2 * half + 2)
                v_.tensor_tensor(Z[par(b, p)][:, k, :], gather_banks(b, p, half)[:, :, :],
                                 X[par(b)][:, k, p * UNIT:(p + 1) * UNIT], ALU.subtract).then_inc(z_done, 1)

            def scale_delta(b, p):
                z = Z[par(b, p)]
                wait(dve, exp_done, b.times(PARTS, p + 1))
                v_.tensor_tensor(z[:, :, :], z[:, :, :], alpha[:, :].unsqueeze(1).to_broadcast([P, KC, UNIT]),
                                 ALU.mult).then_inc(za_done, 1)

            def y_share(b, p):
                if y_shares(b, p) is not None:
                    wait(dve, za_done, b.times(PARTS, p + 1))
                    z = Z[par(b, p)][:, HALF_K:KC, :]
                    v_.tensor_tensor(z, z, X[par(b)][:, HALF_K:KC, p * UNIT:(p + 1) * UNIT], ALU.add
                                     ).then_inc(y_half, 1)

            def add_squares(b, p):
                wait(dve, sq_done, b.times(2 * PARTS, 2 * p + 2))
                v_.tensor_tensor(SQ[:, 2, :], SQ[:, 2, :], SQ[:, 3, :], ALU.add).then_inc(add23_done, 1)
                wait(dve, add23_done, b.times(PARTS, p + 1))
                wait(dve, add01_done, b.times(PARTS, p + 1))
                v_.tensor_tensor(SQ[:, 0, :], SQ[:, 0, :], SQ[:, 2, :], ALU.add).then_inc(s_done, 1)

            def low_sum(b, p):
                wait(dve, sh_done, b.times(PARTS, p + 1))
                wait(dve, one_done, b.times(PARTS, p))
                v_.tensor_tensor(SL[:, :], SQ[:, 0, :], SH[:, :].bitcast(F32), ALU.subtract).then_inc(sl_done, 1)

            def low_clusters(b):
                wait(dve, sumsH_done, b.times(1, 1))
                wait(dve, cop_done, b.times(1, 0))
                v_.tensor_tensor(sumsL[:, :], sumP, sumsH[:, :].bitcast(F32), ALU.subtract).then_inc(sumsL_done, 1)

            def low(b, p):
                wait(dve, hi_done, b.times(PARTS, p + 1))
                if p == PARTS - 1:
                    wait(dve, lo_done, b.times(PARTS, p))
                wait(dve, main_done, b.times(KC * PARTS, KC * (p - 1)))
                j = par(b, p)
                v_.tensor_tensor(YL[j][:, :, :], Z[j][:, :, :], YH[j][:, :, :].bitcast(F32),
                                 ALU.subtract).then_inc(lo_done, 1)

            def body(b):
                nxt = b.plus(1)
                there = b.i is not None or nxt.base < BATCH
                for p in range(PARTS):
                    before, q = previous(b, p)
                    delta(b, p, 0)
                    scale_delta(before, q)
                    if there and p == 0:
                        transpose_unit(nxt, 0)
                    if there and p == 2:
                        transpose_unit(nxt, 2)
                    delta(b, p, 1)
                    y_share(before, q)
                    if there and p == 0:
                        transpose_unit(nxt, 1, (0,))
                    add_squares(b, p)
                    if there and p == 0:
                        transpose_unit(nxt, 1, (1,))
                    low_sum(b, p)
                    if not there:
                        low(before, q)
                    if there and p == 1:
                        argmax(nxt)
                    if there and p == 2:
                        counts(nxt)
                        low_clusters(nxt)
                    if there and p < 2:
                        low(before, q)
                    if there and p == 2:
                        averages(nxt)

            def low_weights(k):
                dve.wait_ge(wh_done, k + 1)
                v_.tensor_tensor(WL[:, k, :], wT(k), WH[:, k, :].bitcast(F32), ALU.subtract).then_inc(wl_done, 1)

            v_.memset(cT[:, :, N:NPAD], 0.0).then_inc(cT_done, 1)
            v_.memset(cstat[:, 0:1], 1.0).then_inc(norm_step, 1)
            v_.memset(oh[:, :, :], 0.0).then_inc(const_done, 1)
            for n in range(N):
                last = v_.memset(weight[:, n:n + 1], float(NPAD - n))
            last.then_inc(const_done, 1)
            dve.wait_ge(norm_step, 4)
            s = lambda c: cstat[:, c:c + 1]
            v_.tensor_scalar(s(2), s(1), EPS, None, ALU.max).then_inc(norm_step, 1)
            dve.wait_ge(norm_step, 5)
            v_.reciprocal(s(3), s(2)).then_inc(norm_step, 1)
            dve.wait_ge(norm_step, 6)
            v_.scalar_tensor_tensor(out=s(4), in0=s(0), scalar=s(3), in1=s(2),
                                    op0=ALU.mult, op1=ALU.add).then_inc(norm_step, 1)
            dve.wait_ge(norm_step, 7)
            v_.tensor_scalar(s(5), s(4), 0.5, EPS, ALU.mult, ALU.max).then_inc(norm_step, 1)
            dve.wait_ge(norm_step, 8)
            v_.reciprocal(s(6), s(5)).then_inc(norm_step, 1)
            b0, b1 = Step(None, 0), Step(None, 1)
            dve.wait_ge(const_done, 7)
            argmax(b0)
            for u in range(PARTS):
                transpose_unit(b0, u)
            for k in range(KC):
                low_weights(k)
            counts(b0)
            low_clusters(b0)
            averages(b0)

            delta(b0, 0, 0)
            delta(b0, 0, 1)
            delta(b0, 1, 0)
            add_squares(b0, 0)
            low_sum(b0, 0)
            delta(b0, 1, 1)
            transpose_unit(b1, 0, (0,))
            z, lower, upper = Z[0], slice(0, HALF_K), slice(HALF_K, KC)
            scale = alpha[:, :].unsqueeze(1).to_broadcast([P, HALF_K, UNIT])
            dve.wait_ge(exp_done, 1)
            v_.tensor_tensor(z[:, lower, :], z[:, lower, :], scale, ALU.mult).then_inc(za_half, 1)
            dve.wait_ge(za_half, 1)
            v_.tensor_tensor(z[:, lower, :], z[:, lower, :], X[0][:, lower, 0:UNIT], ALU.add).then_inc(y_half, 1)
            v_.tensor_tensor(z[:, upper, :], z[:, upper, :], scale, ALU.mult).then_inc(za_done, 1)
            add_squares(b0, 1)
            dve.wait_ge(hi_half, 1)
            v_.tensor_tensor(YL[0][:, lower, :], z[:, lower, :], YH[0][:, lower, :].bitcast(F32), ALU.subtract
                             ).then_inc(lo_half, 1)
            low_sum(b0, 1)
            transpose_unit(b1, 0, (1,))
            argmax(b1)
            delta(b0, 2, 0)
            transpose_unit(b1, 1)
            delta(b0, 2, 1)
            transpose_unit(b1, 2)
            add_squares(b0, 2)
            counts(b1)
            low_clusters(b1)
            low_sum(b0, 2)
            averages(b1)
            images(dve, body)
            end = Step(None, BATCH - 1)
            scale_delta(end, PARTS - 1)
            y_share(end, PARTS - 1)
            low(end, PARTS - 1)

        @block.scalar
        def _(act):
            a_ = nc.scalar

            def square(b, p, half):
                wait(act, z_done, b.times(2 * PARTS, 2 * p + half + 1))
                wait(act, sl_done, b.times(PARTS, p))
                k = slice(2 * half, 2 * half + 2)
                a_.activation(SQ[:, k, :], Z[par(b, p)][:, k, :], ACT.Square).then_inc(sq_done, 1)

            def exp(b, p):
                wait(act, one_done, b.times(PARTS, p + 1))
                wait(act, za_done, b.times(PARTS, p))
                a_.activation(alpha[:, :], sum_bank(b, p)[0], ACT.Exp, scale=-1.0 / C).then_inc(exp_done, 1)

            def high(b, p):
                wait(act, y_done, b.times(PARTS, p + 1))
                if y_shares(b, p) is not None:
                    act.wait_ge(y_half, y_shares(b, p))
                wait(act, main_done, b.times(KC * PARTS, KC * (p - 1)))
                a_.activation(YH[par(b, p)][:, :, :], Z[par(b, p)][:, :, :], ACT.Copy).then_inc(hi_done, 1)

            def high_sum(b, p):
                wait(act, s_done, b.times(PARTS, p + 1))
                wait(act, one_done, b.times(PARTS, p))
                a_.activation(SH[:, :], SQ[:, 0, :], ACT.Copy).then_inc(sh_done, 1)

            def relu(b, p, o):
                if not conv_unit(b, p)[2]:
                    return
                j = par(b, p - LAG)
                wait(act, main_done, b.times(KC * PARTS, KC * (p - LAG) + o + 1))
                if o == 0:
                    fixed = 16 * ((PARTS * b.base + p - LAG) // 2)
                    wait(act, out_done[j], fixed if b.i is None else b.i * (16 * PARTS) + fixed)
                a_.activation(OUT[j][:, o, :], main[:, o % 2, :], ACT.Relu, bias=bcol[:, o:o + 1]
                              ).then_inc(relu_done, 1)

            def copy_sims(b, u):
                wait(act, a_done, b.times(PARTS, u + 1))
                wait(act, simT_done, b.times(1, 0))
                wait(act, g_ready, b.times(1, 0))
                a_.activation(simS[:, u, :, :].rearrange("p t (q i) -> p q t i", q=Q),
                              simP[u].rearrange("p (q t i) -> p q t i", q=Q, t=HALF), ACT.Copy,
                              scale=cstat[:, 6:7]).then_inc(simS_done, 1)

            def copy_onehot(b):
                wait(act, oh_done, b.times(1, 1))
                wait(act, ohP_done, b.times(1, 0))
                a_.activation(oh3[:, :, :, :], oh[:, :, 0:N].unsqueeze(2).to_broadcast(
                    [P, PARTS * TILES, COPIES, N]), ACT.Copy).then_inc(oh3_done, 1)

            def evacuate_onehot(b):
                wait(act, ohP_done, b.times(1, 1))
                wait(act, g_ready, b.times(1, 0))
                wait(act, gat_done, b.times(KC * PARTS, -KC * PARTS))
                a_.activation(ohT[par(b)][:, :], ohP[0:NK, 0:HW], ACT.Copy, accum_out=count[:, :]
                              ).then_inc(ohT_done, 1)

            def copy_sums(b):
                wait(act, c_done, b.times(PARTS, PARTS))
                wait(act, cop_done, b.times(1, 0))
                a_.activation(sumsH[:, :], sumP, ACT.Copy).then_inc(sumsH_done, 1)

            def last_image(b):
                for p in range(PARTS):
                    before, q = previous(b, p)
                    if p == 0:
                        relu(before, q, 3)
                    square(b, p, 0)
                    relu(b, p, 0)
                    square(b, p, 1)
                    relu(b, p, 1)
                    high(before, q)
                    high_sum(b, p)
                    relu(b, p, 2)
                    relu(b, p, 3)
                    exp(b, p)

            def body(b):
                nxt = b.plus(1)
                if b.i is None and nxt.base == BATCH:
                    return last_image(b)
                for p in range(PARTS):
                    before, q = previous(b, p)
                    relu(before, q, 3)
                    square(b, p, 0)
                    if p == 0:
                        copy_sims(nxt, 0)
                    relu(b, p, 0)
                    if p == 2:
                        evacuate_onehot(nxt)
                    square(b, p, 1)
                    if p == 0:
                        copy_sims(nxt, 1)
                    if p == 1:
                        copy_sims(nxt, 2)
                    if p == 0:
                        relu(b, p, 1)
                    high_sum(b, p)
                    if p == 2:
                        copy_sums(nxt)
                    if p == 1:
                        relu(b, p, 1)
                    high(before, q)
                    if p == 2:
                        relu(b, p, 1)
                    relu(b, p, 2)
                    exp(b, p)
                    if p == 1:
                        copy_onehot(nxt)

            act.wait_ge(norm_step, 1)
            act.wait_ge(cT_ps, 1)
            a_.activation(cT[:, :, 0:N], fb[:, 0, 0:KC * N].rearrange("p (k n) -> p k n", k=KC),
                          ACT.Copy).then_inc(cT_done, 1)
            for rows, loaded in zip(column_tiles, c_in):
                act.wait_ge(loaded, 16)
                a_.activation(csq[rows, :], craw[rows, :], ACT.Square, accum_out=cstat[rows, 0:1]
                              ).then_inc(norm_step, 1)
            act.wait_ge(norm_step, 3)
            a_.activation(cstat[:, 1:2], cstat[:, 0:1], ACT.Sqrt).then_inc(norm_step, 1)
            act.wait_ge(norm_step, 9)
            a_.activation(warm[:, :], cstat[:, 6:7], ACT.Exp).then_inc(warm_done, 1)
            b0 = Step(None, 0)
            for u in range(PARTS):
                copy_sims(b0, u)
            for k in range(KC):
                act.wait_ge(wT_ps, k + 1)
                a_.activation(WH[:, k, :], wT(k), ACT.Copy).then_inc(wh_done, 1)
                if k == 0:
                    copy_onehot(b0)
            evacuate_onehot(b0)
            copy_sums(b0)
            act.wait_ge(b_in, 16)

            b1 = b0.plus(1)
            copy_sims(b1, 0)
            square(b0, 0, 0)
            square(b0, 0, 1)
            copy_sims(b1, 1)
            high_sum(b0, 0)
            square(b0, 1, 0)
            exp(b0, 0)
            square(b0, 1, 1)
            copy_sims(b1, 2)
            act.wait_ge(y_half, 1)
            a_.activation(YH[0][:, 0:HALF_K, :], Z[0][:, 0:HALF_K, :], ACT.Copy).then_inc(hi_half, 1)
            high_sum(b0, 1)
            act.wait_ge(y_done, 1)
            a_.activation(YH[0][:, HALF_K:KC, :], Z[0][:, HALF_K:KC, :], ACT.Copy).then_inc(hi_done, 1)
            exp(b0, 1)
            relu(b0, 2, 0)
            relu(b0, 2, 1)
            copy_onehot(b1)
            square(b0, 2, 0)
            relu(b0, 2, 2)
            evacuate_onehot(b1)
            square(b0, 2, 1)
            high_sum(b0, 2)
            copy_sums(b1)
            high(b0, 1)
            exp(b0, 2)
            images(act, body, 3)
            end = Step(None, BATCH)
            relu(end, 0, 0)
            high(end.plus(-1), PARTS - 1)
            for o in (1, 2, 3):
                relu(end, 0, o)
            for o in range(KC):
                relu(end, 1, o)

        @block.tensor
        def _(pe):
            t_ = nc.tensor

            def similarities(b, u):
                loaded = 16 * (b.base // 2 + 1)
                wait(pe, x_in[par(b)][u], loaded if b.i is None else b.i * 16 + loaded)
                wait(pe, ohT_done, b.times(1, 0))
                if u == 2:
                    wait(pe, simS_done, b.times(PARTS, 1))
                rows = X[par(b)]
                for k in range(KC):
                    for h in range(2):
                        toks = rows[:, k, u * UNIT:(u + 1) * UNIT].rearrange("p (q s) -> p q s", q=Q)
                        last = t_.matmul(simP[u][NPAD * h:NPAD * (h + 1), :], cT[:, k, :],
                                         toks[:, :, h * HALF * BLK:(h + 1) * HALF * BLK],
                                         start=(k == 0), stop=(k == KC - 1))
                last.then_inc(a_done, 1)

            def transpose_sims(b):
                wait(pe, simS_done, b.times(PARTS, PARTS))
                wait(pe, g_ready, b.times(1, 0))
                for u in range(PARTS):
                    for t in range(HALF):
                        s = u * HALF + t
                        last = t_.transpose(fb[:, s // 4, (s % 4) * P:(s % 4 + 1) * P], simS[:, u, t, :], ident[:, :])
                last.then_inc(simT_done, 1)

            def slot(u, t):
                return (u * HALF + t % HALF) * 2 + t // HALF

            def transpose_onehot(b):
                wait(pe, oh3_done, b.times(1, 1))
                wait(pe, simS_done, b.times(PARTS, PARTS))
                for u in range(PARTS):
                    for t in range(TILES):
                        dst = ohP[0:NK, u * UNIT:(u + 1) * UNIT].rearrange("n (q t i) -> n q t i", q=Q, t=TILES)
                        last = t_.transpose(dst[:, :, t, :], oh3[:, slot(u, t), :, :].rearrange("p r n -> p (r n)"),
                                            identb[:, :])
                last.then_inc(ohP_done, 1)

            def sum_clusters(b, units):
                if units[0] == 0:
                    wait(pe, oh_done, b.times(1, 1))
                for u in units:
                    wait(pe, tr_done, b.times(PARTS, u + 1))
                    for t in range(HALF):
                        for h in range(2):
                            tile = HALF * h + t
                            last = t_.matmul(sumP[NPAD * h:NPAD * (h + 1), :], oh[:, slot(u, tile), :],
                                             XT[:, u, tile, :], start=(u == 0 and t == 0),
                                             stop=(u == PARTS - 1 and t == HALF - 1))
                    last.then_inc(c_done, 1)

            def add_halves(b):
                wait(pe, sumsH_done, b.times(1, 1))
                wait(pe, sumsL_done, b.times(1, 1))
                rows = select[:, :, :].rearrange("p r n -> p (r n)")
                t_.matmul(copP, rows, sumsH[:, :], start=True, stop=False)
                t_.matmul(copP, rows, sumsL[:, :], start=False, stop=True).then_inc(cop_done, 1)

            def gather(b, p, half):
                wait(pe, g_ready, b.times(1, 1))
                wait(pe, ohT_done, b.times(1, 1))
                banks = gather_banks(b, p, half)
                if half == 0:
                    if sum_bank(*previous(b, p))[1]:
                        wait(pe, exp_done, b.times(PARTS, p))
                    wait(pe, z_done, 1 if b.i is None and (b.base, p) == (0, 1) else b.times(2 * PARTS, 2 * p))
                elif banks is gat:
                    wait(pe, z_done, b.times(2 * PARTS, 2 * p + 1))
                for j in range(2):
                    k = 2 * half + j
                    t_.matmul(banks[:, j, :], G[:, k * P:(k + 1) * P], ohT[par(b)][:, p * UNIT:(p + 1) * UNIT],
                              start=True, stop=True).then_inc(gat_done, 1)

            def sum_squares(b, p):
                wait(pe, z_done, b.times(2 * PARTS, 2 * p + 2))
                wait(pe, sh_done, b.times(PARTS, p + 1))
                wait(pe, sl_done, b.times(PARTS, p + 1))
                t_.matmul(sum_bank(b, p)[0], ones[:, :], SH[:, :], start=True, stop=False)
                t_.matmul(sum_bank(b, p)[0], ones[:, :], SL[:, :], start=False, stop=True).then_inc(one_done, 1)

            def convolve(b, p, o):
                if not conv_unit(b, p)[2]:
                    return
                j = par(b, p - LAG)
                if o == 0:
                    wait(pe, hi_done, b.times(PARTS, p - LAG + 1))
                    wait(pe, lo_done, b.times(PARTS, p - LAG + 1))
                wait(pe, relu_done, b.times(KC * PARTS, KC * (p - LAG) + o - 1))
                cols = slice(o * P, (o + 1) * P)
                for k in range(KC):
                    t_.matmul(main[:, o % 2, :], WH[:, k, cols], YH[j][:, k, :], start=(k == 0), stop=False)
                    t_.matmul(main[:, o % 2, :], WH[:, k, cols], YL[j][:, k, :], start=False, stop=False)
                    last = t_.matmul(main[:, o % 2, :], WL[:, k, cols], YH[j][:, k, :], start=False,
                                     stop=(k == KC - 1))
                last.then_inc(main_done, 1)

            def body(b):
                nxt = b.plus(1)
                there = b.i is not None or nxt.base < BATCH
                for p in range(PARTS):
                    gather(b, p, 0)
                    if there and p == 0:
                        similarities(nxt, 0)
                    convolve(b, p, 0)
                    gather(b, p, 1)
                    if there and p == 0:
                        similarities(nxt, 1)
                    if there and p == 1:
                        similarities(nxt, 2)
                    if there and p == 2:
                        transpose_onehot(nxt)
                        sum_clusters(nxt, range(PARTS))
                    convolve(b, p, 1)
                    if there and p == 1:
                        transpose_sims(nxt)
                    if there and p == 2:
                        add_halves(nxt)
                    convolve(b, p, 2)
                    if there:
                        sum_squares(b, p)
                    convolve(b, p, 3)
                    if not there:
                        sum_squares(b, p)

            pe.wait_ge(ident_done, 5)
            pe.wait_ge(c_in[0], 16)
            for k in range(KC):
                last = t_.transpose(fb[:, 0, k * N:(k + 1) * N], craw[0:N, k * P:(k + 1) * P], ident[0:N, 0:N])
            last.then_inc(cT_ps, 1)
            b0 = Step(None, 0)
            pe.wait_ge(cT_done, 2)
            for u in range(PARTS):
                similarities(b0, u)
            transpose_sims(b0)
            pe.wait_ge(w_in, 16)
            for k in range(KC):
                for o in range(KC):
                    last = t_.transpose(wT(k)[:, o * P:(o + 1) * P], Wraw[:, o, k * P:(k + 1) * P], ident[:, :])
                last.then_inc(wT_ps, 1)
            pe.wait_ge(const_done, 7)
            sum_clusters(b0, [0])
            transpose_onehot(b0)
            sum_clusters(b0, [1, 2])
            add_halves(b0)

            b1 = b0.plus(1)
            similarities(b1, 0)
            pe.wait_ge(wl_done, KC)
            gather(b0, 0, 0)
            gather(b0, 0, 1)
            gather(b0, 1, 0)
            similarities(b1, 1)
            gather(b0, 1, 1)
            sum_squares(b0, 0)
            similarities(b1, 2)
            gather(b0, 2, 0)
            transpose_sims(b1)
            pe.wait_ge(exp_done, 1)

            def high_passes(ks):
                for o in range(2):
                    for k in ks:
                        for weights in (WH, WL):
                            t_.matmul(main[:, o, :], weights[:, k, o * P:(o + 1) * P], YH[0][:, k, :],
                                      start=(k == 0 and weights is WH), stop=False)

            pe.wait_ge(hi_half, 1)
            high_passes(range(HALF_K))
            pe.wait_ge(simS_done, 2 * PARTS)
            sum_squares(b0, 1)
            pe.wait_ge(hi_done, 1)
            high_passes(range(HALF_K, KC))
            pe.wait_ge(lo_half, 1)
            pe.wait_ge(lo_done, 1)
            for o in range(2):
                for k in range(KC):
                    last = t_.matmul(main[:, o, :], WH[:, k, o * P:(o + 1) * P], YL[0][:, k, :],
                                     start=False, stop=(k == KC - 1))
                last.then_inc(main_done, 1)
            convolve(b0, 2, 2)
            gather(b0, 2, 1)
            transpose_onehot(b1)
            sum_clusters(b1, range(PARTS))
            add_halves(b1)
            sum_squares(b0, 2)
            convolve(b0, 2, 3)
            images(pe, body)
            end = Step(None, BATCH)
            for p in range(LAG):
                for o in range(KC):
                    convolve(end, p, o)


def kernel(x, L0_conv_centroids, L0_conv_W, L0_conv_b):
    import concourse.bacc as bacc
    from concourse.bass_utils import run_bass_kernel_spmd

    nc = bacc.Bacc("TRN2", target_bir_lowering=False, num_devices=1)
    x = np.asarray(x)
    shape = x.shape
    arrays = {
        "x": np.ascontiguousarray(x).reshape(BATCH, C, HW),
        "centroids": np.ascontiguousarray(L0_conv_centroids),
        "w": np.ascontiguousarray(L0_conv_W),
        "bias": np.ascontiguousarray(L0_conv_b),
    }
    args = [nc.dram_tensor(n, a.shape, F32, kind="ExternalInput").ap() for n, a in arrays.items()]
    out = nc.dram_tensor("out", (BATCH, C, HW), F32, kind="ExternalOutput").ap()
    build(nc, *args, out)
    got = run_bass_kernel_spmd(nc, [arrays], core_ids=[0])
    return got.results[0]["out"].reshape(shape)
```
